# Optimizing a Trainium2 kernel written in Bass

```python
import numpy as np
import jax
import jax.numpy as jnp

def _softmax(x, axis=-1):
    return jax.nn.softmax(x, axis=axis)

def _gelu(x):
    return jax.nn.gelu(x, approximate=True)

def _silu(x):
    return jax.nn.silu(x)

def _sigmoid(x):
    return jax.nn.sigmoid(x)

def _layernorm(x, axis=-1, eps=1e-05):
    m = jnp.mean(x, axis=axis, keepdims=True)
    v = jnp.var(x, axis=axis, keepdims=True)
    return (x - m) / jnp.sqrt(v + eps)

def _scatter_add(tgt, idx, src, axis=0):
    return tgt.at[idx].add(src)

def _segment_sum(src, seg, n):
    return jax.ops.segment_sum(src, seg, n)
kernel_name = 'mk_rec_standalone_d1_rec_r8_165e10'

def setup_inputs(seed: int=0):
    np.random.seed(seed)
    _w = jnp.asarray

    def _rec_inputs():
        import jax
        import jax.numpy as jnp
        _rk = jax.random.key(seed)
        r_dense_x = -0.00338568 + 1.0005 * jax.random.normal(jax.random.fold_in(_rk, 1), (2048, 13), jnp.float32)
        r_sparse_off = jax.random.randint(jax.random.fold_in(_rk, 2), (26, 2048), 0, 2048, jnp.int32)
        return (r_dense_x, r_sparse_off)
    r_dense_x, r_sparse_off = _rec_inputs()

    def _L0_rec_setup():
        import jax, jax.numpy as jnp
        import numpy as np
        NUM_SPARSE = 26
        EMB_ROWS = 12500
        D = 64
        B = 2048
        NUM_DENSE = 13
        NUM_FEA = NUM_SPARSE + 1

        def _emb_bag_sum(table, idx, off):
            seg = jnp.searchsorted(off, jnp.arange(idx.shape[0]), side='right') - 1
            return jax.ops.segment_sum(table[idx], seg, num_segments=off.shape[0])

        def _forward(dense_x, sparse_off, sparse_idx, emb_tables, W_bot0, b_bot0, W_bot1, b_bot1, W_bot2, b_bot2, W_top0, b_top0, W_top1, b_top1, W_top2, b_top2):
            x = jax.nn.relu(dense_x @ W_bot0 + b_bot0)
            x = jax.nn.relu(x @ W_bot1 + b_bot1)
            x = jax.nn.relu(x @ W_bot2 + b_bot2)
            pooled = jax.vmap(_emb_bag_sum)(emb_tables, sparse_idx, sparse_off)
            T = jnp.concatenate([x[:, None, :], jnp.transpose(pooled, (1, 0, 2))], axis=1)
            Z = jnp.einsum('bik,bjk->bij', T, T)
            li, lj = np.triu_indices(NUM_FEA, k=1)
            z = jnp.concatenate([x, Z[:, li, lj]], axis=1)
            y = jax.nn.relu(z @ W_top0 + b_top0)
            y = jax.nn.relu(y @ W_top1 + b_top1)
            y = y @ W_top2 + b_top2
            return jax.nn.sigmoid(y[:, 0])
        key = jax.random.key(seed)
        ks = jax.random.split(key, 12)
        inp = {}
        inp['dense_x'] = jax.random.normal(ks[0], (B, NUM_DENSE), dtype=jnp.float32)
        inp['sparse_off'] = jnp.tile(jnp.arange(B, dtype=jnp.int64)[None, :], (NUM_SPARSE, 1))
        inp['sparse_idx'] = jax.random.randint(ks[1], (NUM_SPARSE, B), 0, EMB_ROWS, dtype=jnp.int64)
        inp['emb_tables'] = jax.random.uniform(ks[2], (NUM_SPARSE, EMB_ROWS, D), dtype=jnp.float32, minval=-0.01, maxval=0.01)

        def lin(k, fan_in, fan_out):
            lim = (6.0 / (fan_in + fan_out)) ** 0.5
            return jax.random.uniform(k, (fan_in, fan_out), dtype=jnp.float32, minval=-lim, maxval=lim)
        inp['W_bot0'] = lin(ks[3], NUM_DENSE, 512)
        inp['b_bot0'] = jnp.zeros((512,), jnp.float32)
        inp['W_bot1'] = lin(ks[4], 512, 256)
        inp['b_bot1'] = jnp.zeros((256,), jnp.float32)
        inp['W_bot2'] = lin(ks[5], 256, D)
        inp['b_bot2'] = jnp.zeros((D,), jnp.float32)
        inter = NUM_FEA * (NUM_FEA - 1) // 2 + D
        inp['W_top0'] = lin(ks[6], inter, 512)
        inp['b_top0'] = jnp.zeros((512,), jnp.float32)
        inp['W_top1'] = lin(ks[7], 512, 256)
        inp['b_top1'] = jnp.zeros((256,), jnp.float32)
        inp['W_top2'] = lin(ks[8], 256, 1)
        inp['b_top2'] = jnp.zeros((1,), jnp.float32)
        return inp
    _L0_rec_all = _L0_rec_setup()
    _L0_rec_in = {k: v for k, v in _L0_rec_all.items() if k in ('sparse_idx', 'emb_tables', 'W_bot0', 'b_bot0', 'W_bot1', 'b_bot1', 'W_bot2', 'b_bot2', 'W_top0', 'b_top0', 'W_top1', 'b_top1', 'W_top2', 'b_top2')}
    del _L0_rec_all
    return {'r_dense_x': r_dense_x, 'r_sparse_off': r_sparse_off, 'L0_rec_sparse_idx': _L0_rec_in['sparse_idx'], 'L0_rec_emb_tables': _L0_rec_in['emb_tables'], 'L0_rec_W_bot0': _L0_rec_in['W_bot0'], 'L0_rec_b_bot0': _L0_rec_in['b_bot0'], 'L0_rec_W_bot1': _L0_rec_in['W_bot1'], 'L0_rec_b_bot1': _L0_rec_in['b_bot1'], 'L0_rec_W_bot2': _L0_rec_in['W_bot2'], 'L0_rec_b_bot2': _L0_rec_in['b_bot2'], 'L0_rec_W_top0': _L0_rec_in['W_top0'], 'L0_rec_b_top0': _L0_rec_in['b_top0'], 'L0_rec_W_top1': _L0_rec_in['W_top1'], 'L0_rec_b_top1': _L0_rec_in['b_top1'], 'L0_rec_W_top2': _L0_rec_in['W_top2'], 'L0_rec_b_top2': _L0_rec_in['b_top2']}

def reference(r_dense_x, r_sparse_off, L0_rec_sparse_idx, L0_rec_emb_tables, L0_rec_W_bot0, L0_rec_b_bot0, L0_rec_W_bot1, L0_rec_b_bot1, L0_rec_W_bot2, L0_rec_b_bot2, L0_rec_W_top0, L0_rec_b_top0, L0_rec_W_top1, L0_rec_b_top1, L0_rec_W_top2, L0_rec_b_top2):
    import jax
    import jax.numpy as jnp

    def _L0_rec_ref(dense_x, sparse_off, sparse_idx, emb_tables, W_bot0, b_bot0, W_bot1, b_bot1, W_bot2, b_bot2, W_top0, b_top0, W_top1, b_top1, W_top2, b_top2):
        import jax, jax.numpy as jnp
        import numpy as np
        NUM_SPARSE = 26
        EMB_ROWS = 12500
        D = 64
        B = 2048
        NUM_DENSE = 13
        NUM_FEA = NUM_SPARSE + 1

        def _emb_bag_sum(table, idx, off):
            seg = jnp.searchsorted(off, jnp.arange(idx.shape[0]), side='right') - 1
            return jax.ops.segment_sum(table[idx], seg, num_segments=off.shape[0])

        def _forward(dense_x, sparse_off, sparse_idx, emb_tables, W_bot0, b_bot0, W_bot1, b_bot1, W_bot2, b_bot2, W_top0, b_top0, W_top1, b_top1, W_top2, b_top2):
            x = jax.nn.relu(dense_x @ W_bot0 + b_bot0)
            x = jax.nn.relu(x @ W_bot1 + b_bot1)
            x = jax.nn.relu(x @ W_bot2 + b_bot2)
            pooled = jax.vmap(_emb_bag_sum)(emb_tables, sparse_idx, sparse_off)
            T = jnp.concatenate([x[:, None, :], jnp.transpose(pooled, (1, 0, 2))], axis=1)
            Z = jnp.einsum('bik,bjk->bij', T, T)
            li, lj = np.triu_indices(NUM_FEA, k=1)
            z = jnp.concatenate([x, Z[:, li, lj]], axis=1)
            y = jax.nn.relu(z @ W_top0 + b_top0)
            y = jax.nn.relu(y @ W_top1 + b_top1)
            y = y @ W_top2 + b_top2
            return jax.nn.sigmoid(y[:, 0])
        return _forward(dense_x, sparse_off, sparse_idx, emb_tables, W_bot0, b_bot0, W_bot1, b_bot1, W_bot2, b_bot2, W_top0, b_top0, W_top1, b_top1, W_top2, b_top2)
    y = _L0_rec_ref(r_dense_x, r_sparse_off, L0_rec_sparse_idx, L0_rec_emb_tables, L0_rec_W_bot0, L0_rec_b_bot0, L0_rec_W_bot1, L0_rec_b_bot1, L0_rec_W_bot2, L0_rec_b_bot2, L0_rec_W_top0, L0_rec_b_top0, L0_rec_W_top1, L0_rec_b_top1, L0_rec_W_top2, L0_rec_b_top2)
    return y

_drawn_inputs = setup_inputs


def setup_inputs(seed=0):
    import zlib

    import numpy as np

    out = dict(_drawn_inputs(seed))
    spreads = {'L0_rec_b_bot0': (0.0, 0.8),
     'L0_rec_b_bot1': (0.0, 0.8),
     'L0_rec_b_bot2': (0.0, 2.0),
     'L0_rec_b_top0': (0.0, 0.467),
     'L0_rec_b_top1': (0.0, 0.8)}
    factors = {'r_dense_x': 6.814,
     'L0_rec_emb_tables': 8.0,
     'L0_rec_W_bot0': 6.688,
     'L0_rec_W_bot1': 5.025,
     'L0_rec_W_bot2': 5.611,
     'L0_rec_W_top2': 3.123}
    for name, (base, spread) in spreads.items():
        noise = np.random.default_rng([zlib.crc32(name.encode()), seed]).standard_normal(out[name].shape)
        drawn = base * np.exp(spread * noise) if base else spread * noise
        out[name] = jnp.asarray(drawn.astype(out[name].dtype))
    for name, factor in factors.items():
        out[name] = (out[name] * factor).astype(out[name].dtype)
    return out
```

```python
from contextlib import ExitStack

import concourse.bass as bass
from concourse import mybir

F32 = mybir.dt.float32
BF16 = mybir.dt.bfloat16
F16 = mybir.dt.float16
I32 = mybir.dt.int32
ALU = mybir.AluOpType
ACT = mybir.ActivationFunctionType
AX = mybir.AxisListType

P = 128
T = 26
FEA = T + 1
ROWS = 12500
D = 64
B = 2048
NB = B // P
HALF = B // 2
STEPS = 2 * NB - 1
DENSE, H0, H1 = 13, 512, 256
Y0, Y1 = 512, 256
CH = 512
NCH = B // CH
QUAD = 4
NJ = (T + QUAD - 1) // QUAD
FPAD = 32
GB = 64
NG = GB // QUAD
BANK = 512


def build(nc, off, idx, tables, xT, Wb0, bb0, Wb1, bb1, Wb2, bb2, Wt0, bt0, Wt1, bt1, Wt2, bt2, out):
    with ExitStack() as ctx:
        def sb(name, shape, dt=F32):
            return ctx.enter_context(nc.sbuf_tensor(name, shape, dt))

        def sem(name):
            return ctx.enter_context(nc.semaphore(name))

        featT = sb("featT", [P, FEA * HALF])
        zs = sb("zs", [P, NJ * B])
        wt0 = sb("wt0", [P, NJ, Y0])
        N0, N1, N2 = H0, H0 // P * H1, H1 // P * D
        HID0, HID1 = H0 // P * CH, H1 // P * CH
        work = sb("work", [P, N0 + N1 + N2 + HID0 + HID1])
        idx_all = sb("idx_all", [P, (T + 2) * NB], I32)
        idx_slot = sb("idx_slot", [P, 2, NB], I32)
        seg = sb("seg", [P, T * NB])
        iota_bag = sb("iota_bag", [P, B], F16)
        ident = sb("ident", [P, P])
        zeros = sb("zeros", [P, BANK], BF16)
        bias = sb("bias", [P, 16])
        cb0, cb1, cb2, ct0, ct1, ct2 = 0, 4, 6, 7, 11, 13

        staged = work[:, 0:2 * GB * FPAD].rearrange("p (a b f) -> p a b f", a=2, b=GB)
        wb0 = work[0:DENSE, 0:N0]
        wb1 = work[:, N0:N0 + N1].rearrange("p (k n) -> p k n", n=H1)
        wb2 = work[:, N0 + N1:N0 + N1 + N2].rearrange("p (k n) -> p k n", n=D)
        hid0 = work[:, N0 + N1 + N2:N0 + N1 + N2 + HID0].rearrange("p (m c) -> p m c", c=CH)
        hid1 = work[:, N0 + N1 + N2 + HID0:].rearrange("p (m c) -> p m c", c=CH)
        y_out = featT[0:1, 0:B]
        wt1 = featT[:, B:B + Y0 // P * Y1].rearrange("p (k n) -> p k n", n=Y1)
        wt2 = featT[:, 2 * B:2 * B + Y1 // P]
        top0 = featT[:, 3 * B:3 * B + Y0 // P * CH].rearrange("p (m c) -> p m c", c=CH)
        top1 = featT[:, 4 * B:4 * B + Y1 // P * CH].rearrange("p (m c) -> p m c", c=CH)
        TN = T * NB
        lt_hi = work[:, 0:TN * NB // 2].bitcast(BF16).rearrange("p (c t h) -> p c t h", c=NB, t=T)
        small = wt0[:, :, :].rearrange("p n y -> p (n y)")
        thr_i = small[:, 0:TN].bitcast(I32)
        lo_i = small[:, TN:2 * TN].bitcast(I32)
        hi_i = small[:, 2 * TN:3 * TN].bitcast(I32)
        lo_f = small[:, 3 * TN:4 * TN]
        hi_f = small[:, 4 * TN:5 * TN]
        idx_raw = small[:, 5 * TN:6 * TN].bitcast(I32)
        idx_base = small[:, 6 * TN:7 * TN].bitcast(I32)
        tiny = small[:, 7 * TN:8 * TN]
        iota_h = tiny[:, 0:16]
        iota_l = tiny[:, 16:80].bitcast(BF16)
        ones = tiny[:, 80:144].bitcast(BF16)
        pick_last = tiny[:, 144:144 + STEPS]
        iota_s = tiny[:, 176:177]
        iota_k = tiny[0:STEPS, 180:196]
        k_of_step = tiny[0:STEPS, 200:200 + T]
        k_int = tiny[0:T, 228:260].bitcast(I32)
        end_i = thr_i[0:STEPS, :]
        end_b = lo_i[0:STEPS, :]
        end_f = hi_f[0:STEPS, :]
        end_m = lo_f[0:STEPS, :]
        passed = small[0:STEPS, 5 * TN:6 * TN]
        at = [0]

        def part(n):
            at[0] += n
            return zs[:, at[0] - n:at[0]]

        rows = part(2 * NB * D).rearrange("p (a r) -> p a r", a=2)
        x_sb = part(B)[0:DENSE, :]
        member = part(STEPS * P).rearrange("p (s b) -> p s b", b=P)
        pooled = part(2 * NB * D).rearrange("p (a r) -> p a r", a=2)
        thr = part(B + 1)[0:T, :]
        k_row = thr[0:1, 0:T * 32].bitcast(I32)
        eq_hi = zs[:, 2 * NB * D + B:2 * NB * D + B + TN * NB // 2].bitcast(BF16)
        eq_hi = eq_hi.rearrange("p (c t h) -> p c t h", c=NB, t=T)
        thr_raw = zs[0:T, (NJ - 1) * B:NJ * B].bitcast(I32)
        off0 = sb("off0", [T, 1])
        ge_flat = featT[:, HALF:FEA * HALF].bitcast(BF16)
        ge_lo = ge_flat.rearrange("p (t c l) -> p t c l", t=T, c=NB)

        ps = ctx.enter_context(nc.psum_tensor("ps", [P, 8 * BANK], F32))

        def bank(n, k=1):
            return ps[:, n * BANK:(n + k) * BANK]

        off_in, idx_in, w_in, x_in = sem("off_in"), sem("idx_in"), sem("w_in"), sem("x_in")
        top_in = sem("top_in")
        consts_ready = sem("consts_ready")
        pool_step = sem("pool_step")
        dve_step = sem("dve_step")
        idx_ready = sem("idx_ready")
        thr_ready = sem("thr_ready")
        thr_turned = sem("thr_turned")
        hot_ready = sem("hot_ready")
        counts_ready = sem("counts_ready")
        seg_ready = sem("seg_ready")
        ends_ready = sem("ends_ready")
        ksteps_ready = sem("ksteps_ready")
        ksteps_turned = sem("ksteps_turned")
        kint_ready = sem("kint_ready")
        krow_in = sem("krow_in")
        slot_ready = sem("slot_ready")
        rows_in = [sem("rows_in_a"), sem("rows_in_b")]
        member_ready = sem("member_ready")
        member_used = sem("member_used")
        acc_read = sem("acc_read")
        turned = sem("turned")
        turned_read = sem("turned_read")
        mlp_made = sem("mlp_made")
        mlp_read = sem("mlp_read")
        pads_ready = sem("pads_ready")
        staged_ready = sem("staged_ready")
        gram_made = sem("gram_made")
        gram_act = sem("gram_act")
        gram_dve = sem("gram_dve")
        top_made = sem("top_made")
        top_read = sem("top_read")
        out_done = sem("out_done")
        pool_held, dve_held, pe_held = sem("pool_held"), sem("dve_held"), sem("pe_held")

        block = ctx.enter_context(nc.Block())

        def stair_registers(engine_type, t):
            _, ks = nc.values_load_multi_w_load_instructions(
                k_row[0:1, bass.ds(t * 32, STEPS)], engines=(engine_type,), min_val=0, max_val=NB - 1,
                skip_runtime_bounds_check_because="k is a count of at most 15 blocks")
            return [nc.s_assert_within(k, max(0, s - NB + 1), min(NB - 1, s), skip_runtime_bounds_check_because="the staircase stays within the blocks")
                    for s, k in enumerate(ks)]

        def gram_share(eng, copy, cs, done):
            with eng.Fori(0, HALF // GB) as mb:
                for half in range(2):
                    eng.wait_ge(gram_made, 2 * mb + half + 5)
                    prod = bank(4 * half, 4).rearrange("p (g j) -> p g j", g=NG)
                    for c in cs:
                        for m in range(QUAD):
                            n = NJ if 1 + m + QUAD * (NJ - 1) < FEA else NJ - 1
                            src = prod[32 * c:32 * c + 32, :, c * FEA + 1 + m:c * FEA + 2 + m + QUAD * (n - 1):QUAD]
                            z = zs[32 * m:32 * m + 32, :].rearrange("p (n b) -> p n b", n=NJ)
                            z = z[:, 0:n, bass.ds(half * HALF + c + mb * GB, NG, QUAD)]
                            last = copy(z.rearrange("p n g -> p g n"), src)
                    last.then_inc(done, 1)

        @block.sync
        def _(sp):
            sp.dma_start(idx_raw, idx).then_inc(idx_in, 16)
            sp.dma_start(thr_raw, off).then_inc(off_in, 16)
            sp.dma_start(x_sb[:, :], xT).then_inc(x_in, 16)
            for col, vec, n, w in ((cb0, bb0, H0, P), (cb1, bb1, H1, P), (cb2, bb2, D, D),
                                   (ct0, bt0, Y0, P), (ct1, bt1, Y1, P), (ct2, bt2, 1, 1)):
                sp.dma_start(bias[0:w, col:col + n // w], vec).then_inc(w_in, 16)
            sp.wait_ge(counts_ready, 1)
            sp.dma_start(wb0, Wb0).then_inc(x_in, 16)
            sp.dma_start(wb1, Wb1.rearrange("(k p) n -> p k n", p=P)).then_inc(x_in, 16)
            sp.dma_start(wb2, Wb2.rearrange("(k p) n -> p k n", p=P)).then_inc(x_in, 16)
            sp.wait_ge(kint_ready, 1)
            sp.dma_start(k_row[0:1, :].rearrange("a (t s) -> a t s", t=T), k_int).then_inc(krow_in, 16)
            sp.wait_ge(krow_in, 16)
            sp.dma_start(wt0[:, :, :], Wt0).then_inc(top_in, 16)
            sp.wait_ge(staged_ready, HALF // GB)
            sp.dma_start(wt1, Wt1.rearrange("(k p) n -> p k n", p=P)).then_inc(top_in, 16)
            sp.dma_start(wt2, Wt2).then_inc(top_in, 16)
            sp.wait_ge(top_read, NCH * 7)
            sp.dma_start(out, y_out[0:1, :]).then_inc(out_done, 16)
            sp.wait_ge(out_done, 16)

        W_IN = 6 * 16

        @block.gpsimd
        def _(pool):
            g = nc.gpsimd
            g.iota(idx_base, [[ROWS, T], [0, NB]], base=0, channel_multiplier=0).then_inc(consts_ready, 1)
            g.memset(ident[:, :], 0.0).then_inc(pool_step, 1)
            g.memset(pick_last, 0.0).then_inc(pool_step, 1)
            pool.wait_ge(pool_step, 2)
            g.affine_select(out=ident[:, :], in_=ident[:, :], compare_op=ALU.not_equal, fill=1.0, base=0,
                            pattern=[[-1, P]], channel_multiplier=1).then_inc(consts_ready, 1)
            g.affine_select(out=pick_last, in_=pick_last, compare_op=ALU.not_equal, fill=1.0, base=-(P - 1),
                            pattern=[[0, STEPS]], channel_multiplier=1).then_inc(consts_ready, 1)
            g.iota(iota_l, [[1, P]], base=0, channel_multiplier=0,
                   allow_small_or_imprecise_dtypes=True).then_inc(consts_ready, 1)
            g.iota(iota_h, [[1, NB]], base=0, channel_multiplier=0,
                   allow_small_or_imprecise_dtypes=True).then_inc(consts_ready, 1)
            g.iota(iota_bag[:, :], [[1, B]], base=0, channel_multiplier=0,
                   allow_small_or_imprecise_dtypes=True).then_inc(consts_ready, 1)
            g.iota(iota_s, [[0, 1]], base=0, channel_multiplier=1,
                   allow_small_or_imprecise_dtypes=True).then_inc(consts_ready, 1)
            g.iota(iota_k, [[1, NB]], base=0, channel_multiplier=0,
                   allow_small_or_imprecise_dtypes=True).then_inc(consts_ready, 1)
            g.memset(ones, 1.0).then_inc(consts_ready, 1)
            g.memset(zeros[:, :], 0.0).then_inc(consts_ready, 1)
            table_rows = tables.rearrange("t r d -> (t r) d")
            with pool.Fori(0, T // 2) as it:
                for par in range(2):
                    pool.wait_ge(slot_ready, 2 * it + par + 1)
                    pool.sem_inc(pool_held, 1)
                    for k in range(NB):
                        g.indirect_dma_start(
                            rows[:, par, k * D:(k + 1) * D], None, table_rows,
                            bass.IndirectOffsetOnAxis(ap=idx_slot[:, par, k:k + 1], axis=0),
                        ).then_inc(rows_in[par], 16)

            pool.wait_ge(pads_ready, 1)
            pool.wait_ge(turned_read, T + 1)
            by_bag = featT[:, :].rearrange("p (f b) -> p f b", f=FEA)
            with pool.Fori(0, HALF // GB // 2) as mb2:
                for slot in range(2):
                    pool.wait_ge(gram_made, 4 * mb2 + 2 * slot + 2)
                    g.tensor_copy(staged[:, slot, :, 0:FEA],
                                  by_bag[:, :, bass.ds(mb2 * (2 * GB) + slot * GB, GB)].rearrange("p f b -> p b f"),
                                  ).then_inc(staged_ready, 1)

        CONSTS = 10

        @block.vector
        def _(dve):
            v = nc.vector
            chain = [0]

            def link(ins):
                chain[0] += 1
                ins.then_inc(dve_step, 1)
                dve.wait_ge(dve_step, chain[0])

            dve.wait_ge(idx_in, 16)
            dve.wait_ge(consts_ready, 1)
            v.memset(idx_all[:, T * NB:], 0)
            v.tensor_tensor(idx_all[:, 0:T * NB], idx_raw, idx_base, ALU.add).then_inc(idx_ready, 1)

            dve.wait_ge(off_in, 16)
            v.memset(thr[:, 0:1], 0.0)
            v.memset(thr[:, B:B + 1], float(B))
            v.tensor_copy(off0[:, :], thr_raw[:, 0:1])
            link(v.tensor_copy(thr[:, 1:B], thr_raw[:, 1:B]))
            s = B // 2
            while s:
                n = B // (2 * s)
                mid = thr[:, s:s + (n - 1) * 2 * s + 1:2 * s]
                left = thr[:, 0:(n - 1) * 2 * s + 1:2 * s]
                right = thr[:, 2 * s:2 * s + (n - 1) * 2 * s + 1:2 * s]
                link(v.tensor_tensor(mid, mid, left, ALU.max))
                link(v.tensor_tensor(mid, mid, right, ALU.min))
                s //= 2
            link(v.tensor_scalar(off0[:, :], off0[:, :], 0.0, None, ALU.max))
            v.tensor_tensor(thr[:, 0:1], off0[:, :], thr[:, 1:2], ALU.min).then_inc(thr_ready, 1)

            dve.wait_ge(consts_ready, CONSTS)
            dve.wait_ge(thr_turned, 1)
            link(v.tensor_copy(thr_i, bank(0)[:, 0:T * NB]))
            link(v.tensor_scalar(lo_i, thr_i, P - 1, None, ALU.bitwise_and))
            link(v.tensor_scalar(hi_i, thr_i, 7, None, ALU.arith_shift_right))
            link(v.tensor_copy(lo_f, lo_i))
            link(v.tensor_copy(hi_f, hi_i))
            hi_b = hi_f.rearrange("p (c t h) -> p c t h", c=NB, h=1).broadcast_to([P, NB, T, NB])
            io_b = iota_h.rearrange("p (a b h) -> p a b h", a=1, b=1).broadcast_to([P, NB, T, NB])
            v.tensor_tensor(eq_hi, hi_b, io_b, ALU.is_equal)
            v.tensor_tensor(lt_hi, hi_b, io_b, ALU.is_lt)
            with dve.Fori(0, T) as t:
                for c in range(NB):
                    last = v.tensor_scalar(
                        ge_flat[:, bass.ds(t * (NB * P) + c * P, P)],
                        iota_l, lo_f[:, bass.ds(t + c * T, 1)], None, ALU.is_ge)
                last.then_inc(hot_ready, 1)

            dve.wait_ge(counts_ready, 1)
            v.tensor_scalar(seg[:, :], bank(1)[:, 0:T * NB], -1.0, None, ALU.add).then_inc(seg_ready, 1)
            dve.wait_ge(ends_ready, 1)
            link(v.tensor_scalar(end_i, bank(2)[0:STEPS, 0:T * NB], 0.0, None, ALU.max))
            link(v.tensor_scalar(end_b, end_i, 7, None, ALU.arith_shift_right))
            link(v.tensor_copy(end_f, end_b))
            link(v.tensor_tensor(end_m.rearrange("p (t k) -> p t k", t=T),
                                 end_f.rearrange("p (t k) -> p t k", t=T),
                                 iota_k.rearrange("p (t k) -> p t k", t=1).broadcast_to([STEPS, T, NB]), ALU.add))
            link(v.tensor_scalar(passed, end_m, iota_s[0:STEPS, :], None, ALU.is_lt))
            v.tensor_reduce(k_of_step, passed.rearrange("p (t k) -> p t k", t=T)[:, :, 0:NB - 1],
                            AX.X, ALU.add).then_inc(ksteps_ready, 1)
            dve.wait_ge(ksteps_turned, 1)
            v.memset(k_int, 0).then_inc(dve_step, 1)
            chain[0] += 1
            dve.wait_ge(dve_step, chain[0])
            v.tensor_copy(k_int[:, 0:STEPS], bank(3)[0:T, 0:STEPS]).then_inc(kint_ready, 1)

            dve.wait_ge(krow_in, 16)
            with dve.Fori(0, T // 2) as it:
                for par in range(2):
                    t = 2 * it + par
                    ks = stair_registers(mybir.EngineType.DVE, t)
                    for s in range(STEPS):
                        if s % 8 == 0:
                            dve.wait_ge(member_used, t * STEPS + min(s + 8, STEPS))
                            dve.sem_inc(dve_held, 1)
                        v.tensor_scalar(member[:, s, :], iota_bag[:, bass.ds((s - ks[s]) * P, P)],
                                        seg[:, bass.ds(t * NB + ks[s], 1)], None,
                                        ALU.is_equal).then_inc(member_ready, 1)

            dve.wait_ge(mlp_read, 7 * NCH + 1)
            v.memset(work[:, 0:2 * GB * FPAD], 0.0).then_inc(pads_ready, 1)
            gram_share(dve, v.tensor_copy, (2, 3), gram_dve)

        @block.scalar
        def _(act):
            a = nc.scalar

            def hand_indices(par, t):
                a.copy(idx_slot[:, par, :], idx_all[:, bass.ds(t * NB, NB)]).then_inc(slot_ready, 1)

            def mlp_chunk(c, half):
                n = c + (2 * half)
                for i in range(7):
                    act.wait_ge(mlp_made, 7 * n + i + 1)
                    src = bank(6 + i % 2)
                    if i < 4:
                        a.activation(hid0[:, i, :], src, ACT.Relu, bias=bias[:, cb0 + i:cb0 + i + 1]).then_inc(mlp_read, 1)
                    elif i < 6:
                        a.activation(hid1[:, i - 4, :], src, ACT.Relu,
                                     bias=bias[:, cb1 + i - 4:cb1 + i - 3]).then_inc(mlp_read, 1)
                    else:
                        a.activation(zs[D:P, bass.ds((NJ - 1) * B + half * HALF + c * CH, CH)], src[0:D, :],
                                     ACT.Relu, bias=bias[0:D, cb2:cb2 + 1])
                        a.activation(featT[D * half:D * half + D, bass.ds(c * CH, CH)], src[0:D, :],
                                     ACT.Relu, bias=bias[0:D, cb2:cb2 + 1]).then_inc(mlp_read, 1)

            def table(par, t):
                act.wait_ge(member_used, t * STEPS + 2 * STEPS)
                a.copy(pooled[:, par, :].rearrange("p (j h d) -> p h j d", h=2, d=D),
                       bank(2 * par, 2).rearrange("p (h j d) -> p h j d", h=2, d=D)).then_inc(acc_read, 1)
                hand_indices(par, t + 2)
                act.wait_ge(turned, t + 1)
                a.copy(featT[:, bass.ds((t + 1) * HALF, HALF)], bank(4, 2)).then_inc(turned_read, 1)

            act.wait_ge(idx_ready, 1)
            hand_indices(0, 0)
            hand_indices(1, 1)
            act.wait_ge(w_in, W_IN)
            act.wait_ge(kint_ready, 1)
            act.wait_ge(krow_in, 16)
            for half in range(2):
                with act.Fori(0, 2) as c:
                    mlp_chunk(c, half)
                    for par in range(2):
                        table(par, 4 * half + 2 * c + par)
            with act.Fori(4, T // 2) as it:
                for par in range(2):
                    table(par, 2 * it + par)

            gram_share(act, a.copy, (0, 1), gram_act)

            with act.Fori(0, NCH) as c:
                for i in range(6):
                    act.wait_ge(top_made, 7 * c + i + 1)
                    if i < 4:
                        a.activation(top0[:, i, :], bank(i), ACT.Relu, bias=bias[:, ct0 + i:ct0 + i + 1]).then_inc(top_read, 1)
                    else:
                        a.activation(top1[:, i - 4, :], bank(i), ACT.Relu,
                                     bias=bias[:, ct1 + i - 4:ct1 + i - 3]).then_inc(top_read, 1)
                act.wait_ge(top_made, 7 * c + 7)
                a.activation(y_out[0:1, bass.ds(c * CH, CH)], bank(6)[0:1, :], ACT.Sigmoid,
                             bias=bias[0:1, ct2:ct2 + 1]).then_inc(top_read, 1)

        @block.tensor
        def _(pe):
            mm = nc.tensor.matmul
            pe.sem_inc(member_used, STEPS)
            pe.sem_inc(acc_read, 2)
            pe.sem_inc(turned_read, 1)
            pe.sem_inc(mlp_read, 1)
            pe.sem_inc(gram_made, 4)
            pe.sem_inc(gram_act, 2)
            pe.sem_inc(gram_dve, 2)

            pe.wait_ge(consts_ready, CONSTS)
            pe.wait_ge(thr_ready, 1)
            for c in range(NB):
                last = nc.tensor.transpose(bank(0)[:, c * T:(c + 1) * T], thr[:, c * P:(c + 1) * P], ident[0:T, 0:T])
            last.then_inc(thr_turned, 1)

            pe.wait_ge(hot_ready, 1)
            for c in range(NB):
                mm(bank(1)[:, 0:T * NB], ones, lt_hi[:, c, :, :].rearrange("p t h -> p (t h)"),
                   start=(c == 0), stop=False, skip_group_check=True)
            for t in range(T):
                pe.wait_ge(hot_ready, t + 1)
                for c in range(NB):
                    last = mm(bank(1)[:, t * NB:(t + 1) * NB], ge_lo[:, t, c, :], eq_hi[:, c, t, :],
                              start=False, stop=(c == NB - 1), skip_group_check=True)
            last.then_inc(counts_ready, 1)
            pe.wait_ge(seg_ready, 1)
            mm(bank(2)[0:STEPS, 0:T * NB], pick_last, seg[:, :], start=True, stop=True).then_inc(ends_ready, 1)
            pe.wait_ge(ksteps_ready, 1)
            nc.tensor.transpose(bank(3)[0:T, 0:STEPS], k_of_step, ident[0:STEPS, 0:STEPS]).then_inc(ksteps_turned, 1)
            pe.wait_ge(krow_in, 16)

            def mlp_chunk(c, half):
                n7 = 7 * c + 14 * half
                for i in range(7):
                    pe.wait_ge(mlp_read, n7 + (1, 1, 2, 3, 5, 5, 7)[i])
                    if i < 4:
                        pe.sem_inc(pe_held, 1)
                    dst = bank(6 + i % 2)
                    if i < 4:
                        mm(dst, wb0[:, i * P:(i + 1) * P], x_sb[:, bass.ds(half * HALF + c * CH, CH)],
                           start=True, stop=True).then_inc(mlp_made, 1)
                    elif i < 6:
                        for k in range(H0 // P):
                            last = mm(dst, wb1[:, k, (i - 4) * P:(i - 3) * P], hid0[:, k, :],
                                      start=(k == 0), stop=(k == H0 // P - 1))
                        last.then_inc(mlp_made, 1)
                    else:
                        for k in range(H1 // P):
                            last = mm(dst[0:D, :], wb2[:, k, :], hid1[:, k, :], start=(k == 0), stop=(k == H1 // P - 1))
                        last.then_inc(mlp_made, 1)

            def table(par, it, t):
                ks = stair_registers(mybir.EngineType.PE, t)
                pe.wait_ge(acc_read, t + 1)
                for h in range(2):
                    mm(bank(2 * par + h), zeros[:, 0:P], zeros[:, :], start=True, stop=False, skip_group_check=True)
                pe.wait_ge(rows_in[par], 256 * it + 256)
                for s in range(STEPS):
                    pe.wait_ge(member_ready, t * STEPS + s + 1)
                    last = mm(ps[:, bass.ds(2 * par * BANK + (s - ks[s]) * D, D)], member[:, s, :],
                              rows[:, par, bass.ds(ks[s] * D, D)], start=False, stop=(s == STEPS - 1),
                              skip_group_check=True).then_inc(member_used, 1)
                pe.wait_ge(turned_read, t + 1)
                pe.wait_ge(acc_read, t + 3)
                for j in range(NB // 2):
                    last = nc.tensor.transpose(bank(4, 2)[:, j * P:(j + 1) * P], pooled[:, par, j * P:(j + 1) * P], ident[:, :])
                last.then_inc(turned, 1)

            pe.wait_ge(x_in, 64)
            pe.wait_ge(w_in, W_IN)
            for half in range(2):
                with pe.Fori(0, 2) as c:
                    mlp_chunk(c, half)
                    for par in range(2):
                        table(par, 2 * half + c, 4 * half + 2 * c + par)
            with pe.Fori(4, T // 2) as it:
                for par in range(2):
                    table(par, it, 2 * it + par)

            pe.wait_ge(turned_read, T + 1)
            with pe.Fori(0, HALF // GB // 2) as mb2:
                for slot in range(2):
                    pe.wait_ge(staged_ready, 2 * mb2 + slot + 1)
                    for half in range(2):
                        pe.wait_ge(gram_act, 4 * mb2 + 2 * slot + half + 1)
                        pe.wait_ge(gram_dve, 4 * mb2 + 2 * slot + half + 1)
                        for gr in range(NG):
                            four = staged[D * half:D * half + D, slot, QUAD * gr:QUAD * gr + QUAD, :]
                            last = mm(bank(4 * half, 4)[:, gr * P:gr * P + QUAD * FEA],
                                      four.rearrange("p b f -> p (b f)"), four[:, :, 0:FEA], start=True, stop=True)
                        last.then_inc(gram_made, 1)

            pe.wait_ge(top_in, 48)
            pe.wait_ge(gram_act, 2 * HALF // GB + 2)
            pe.wait_ge(gram_dve, 2 * HALF // GB + 2)
            with pe.Fori(0, NCH) as c:
                for i in range(7):
                    if i < 4:
                        for n in range(NJ):
                            last = mm(bank(i), wt0[:, n, i * P:(i + 1) * P], zs[:, bass.ds(n * B + c * CH, CH)],
                                      start=(n == 0), stop=(n == NJ - 1))
                    elif i < 6:
                        pe.wait_ge(top_read, 7 * c + 4)
                        for k in range(Y0 // P):
                            last = mm(bank(i), wt1[:, k, (i - 4) * P:(i - 3) * P], top0[:, k, :],
                                      start=(k == 0), stop=(k == Y0 // P - 1))
                    else:
                        pe.wait_ge(top_read, 7 * c + 6)
                        for k in range(Y1 // P):
                            last = mm(bank(i)[0:1, :], wt2[:, k:k + 1], top1[:, k, :], start=(k == 0),
                                      stop=(k == Y1 // P - 1))
                    last.then_inc(top_made, 1)


_INS = ["off", "idx", "tables", "xT", "Wb0", "bb0", "Wb1", "bb1", "Wb2", "bb2", "Wt0", "bt0", "Wt1", "bt1", "Wt2", "bt2"]


def kernel(r_dense_x, r_sparse_off, L0_rec_sparse_idx, L0_rec_emb_tables, L0_rec_W_bot0, L0_rec_b_bot0,
           L0_rec_W_bot1, L0_rec_b_bot1, L0_rec_W_bot2, L0_rec_b_bot2, L0_rec_W_top0, L0_rec_b_top0,
           L0_rec_W_top1, L0_rec_b_top1, L0_rec_W_top2, L0_rec_b_top2):
    import numpy as np
    import concourse.bacc as bacc
    from concourse.bass_utils import run_bass_kernel_spmd as run

    def column(vec, w):
        return np.ascontiguousarray(np.asarray(vec).reshape(-1, w).T)

    w0 = np.asarray(L0_rec_W_top0)
    wt0 = np.zeros((P, NJ, Y0), w0.dtype)
    row = D
    for i in range(FEA):
        for j in range(i + 1, FEA):
            wt0[32 * ((j - 1) % QUAD) + i, (j - 1) // QUAD] = w0[row]
            row += 1
    wt0[D:P, NJ - 1] = w0[0:D]
    data = {
        "off": np.asarray(r_sparse_off),
        "idx": np.ascontiguousarray(np.asarray(L0_rec_sparse_idx).reshape(T, NB, P).transpose(2, 0, 1).reshape(P, T * NB)),
        "tables": np.asarray(L0_rec_emb_tables),
        "xT": np.ascontiguousarray(np.asarray(r_dense_x).T),
        "Wb0": np.asarray(L0_rec_W_bot0), "bb0": column(L0_rec_b_bot0, P),
        "Wb1": np.asarray(L0_rec_W_bot1), "bb1": column(L0_rec_b_bot1, P),
        "Wb2": np.asarray(L0_rec_W_bot2), "bb2": column(L0_rec_b_bot2, D),
        "Wt0": wt0, "bt0": column(L0_rec_b_top0, P),
        "Wt1": np.asarray(L0_rec_W_top1), "bt1": column(L0_rec_b_top1, P),
        "Wt2": column(L0_rec_W_top2, P), "bt2": column(L0_rec_b_top2, 1),
    }
    nc = bacc.Bacc("TRN2", target_bir_lowering=False, num_devices=1)
    args = [nc.dram_tensor(n, data[n].shape, mybir.dt.from_np(data[n].dtype), kind="ExternalInput").ap() for n in _INS]
    out = nc.dram_tensor("out", (1, B), F32, kind="ExternalOutput").ap()
    build(nc, *args, out)
    result = run(nc, [data], core_ids=[0])
    return result.results[0]["out"].reshape(B)
```

```python
from contextlib import ExitStack

import concourse.bass as bass
from concourse import mybir

F32 = mybir.dt.float32
BF16 = mybir.dt.bfloat16
F16 = mybir.dt.float16
I32 = mybir.dt.int32
ALU = mybir.AluOpType
ACT = mybir.ActivationFunctionType
AX = mybir.AxisListType

P = 128
T = 26
FEA = T + 1
ROWS = 12500
D = 64
B = 2048
NB = B // P
HALF = B // 2
STEPS = 2 * NB - 1
DENSE, H0, H1 = 13, 512, 256
Y0, Y1 = 512, 256
CH = 512
NCH = B // CH
HCH = CH // 2
QUAD = 4
NJ = (T + QUAD - 1) // QUAD
FPAD = 32
SUB = 4
UNITS = HCH // (SUB * QUAD)
GB = 2 * SUB * QUAD
BANK = 512
BEATS = 8
LAG = NB - 2


def build(nc, off, idx, tables, xT, Wb0, bb0, Wb1, bb1, Wb2, bb2, Wt0, bt0, Wt1, bt1, Wt2, bt2, out):
    with ExitStack() as ctx:
        def sb(name, shape, dt=F32):
            return ctx.enter_context(nc.sbuf_tensor(name, shape, dt))

        def sem(name):
            return ctx.enter_context(nc.semaphore(name))

        featT = sb("featT", [P, FEA * HALF])
        wt0 = sb("wt0", [P, NJ, Y0])
        z = sb("z", [P, 2, NJ, 2, HCH])
        staged = sb("staged", [P, 2, GB, FPAD])
        NR = NB * D
        loop = sb("loop", [P, 2 * NR + 16 * P + NR])
        ge_lo = sb("ge_lo", [P, NB, P], BF16)
        eq_hi = sb("eq_hi", [P, NB, NB], BF16)
        lt_hi = sb("lt_hi", [P, NB, NB], BF16)
        lo_all = sb("lo_all", [P, (T + 1) * NB], F16)
        hi_all = sb("hi_all", [P, (T + 1) * NB], F16)
        lo_slot = sb("lo_slot", [P, NB])
        idx_all = sb("idx_all", [P, (T + 2) * NB], I32)
        idx_slot = sb("idx_slot", [P, 2, NB], I32)
        seg = sb("seg", [P, 2, NB])
        k_row = sb("k_row", [1, T * 32], I32)
        ident = sb("ident", [P, P])
        iota_l = sb("iota_l", [P, P], BF16)
        ones = sb("ones", [P, P], BF16)
        zeros = sb("zeros", [P, P], BF16)
        iota_h = sb("iota_h", [P, NB])
        bag_base = sb("bag_base", [P, NB])
        wt2 = sb("wt2", [P, Y1 // P])
        bias = sb("bias", [P, 16])
        cb0, cb1, cb2, ct0, ct1, ct2 = 0, 4, 6, 7, 11, 13

        def parts(tile, *widths):
            at, found = 0, []
            for w in widths:
                found.append(tile[:, at:at + w])
                at += w
            return found

        rows, member, pooled = parts(loop, 2 * NR, 16 * P, NR)
        rows = rows.rearrange("p (a r) -> p a r", a=2)
        member = member.rearrange("p (s b) -> p s b", b=P)
        top0, top1, wt1, y_out = parts(loop, Y0 // P * CH, Y1 // P * CH, Y0 // P * Y1, 2 * CH)
        top0 = top0.rearrange("p (m c) -> p m c", c=CH)
        top1 = top1.rearrange("p (m c) -> p m c", c=CH)
        wt1 = wt1.rearrange("p (k n) -> p k n", n=Y1)
        early = z[:, :, :, :, :].rearrange("p s n h b -> p (s n h b)")
        wb0, wb1, wb2, hid0, hid1, x_sb = parts(early, H0, H0 // P * H1, H1 // P * D, H0 // P * CH, H1 // P * CH, B)
        wb1 = wb1.rearrange("p (k n) -> p k n", n=H1)
        wb2 = wb2.rearrange("p (k n) -> p k n", n=D)
        hid0 = hid0.rearrange("p (m c) -> p m c", c=CH)
        hid1 = hid1.rearrange("p (m c) -> p m c", c=CH)
        wb0, x_sb = wb0[0:DENSE, :], x_sb[0:DENSE, :]
        late = featT[:, (FEA - 8) * HALF:]
        TN = T * NB
        PW = STEPS + LAG
        (thr_raw, thr_i, lo_i, hi_i, idx_raw, idx_base, passed, block_end, k_of_step, k_int, off0, thr) = parts(
            late, B, TN, TN, TN, TN, TN, (NB - 1) * PW, NB, 32, 32, 1, B + 1)
        thr_raw, thr_i, lo_i, hi_i, idx_raw, idx_base, k_int = (
            x.bitcast(I32) for x in (thr_raw, thr_i, lo_i, hi_i, idx_raw, idx_base, k_int))
        thr_raw, passed, k_of_step, k_int, off0, thr = (x[0:T, :] for x in (thr_raw, passed, k_of_step, k_int, off0, thr))

        ps = ctx.enter_context(nc.psum_tensor("ps", [P, 8 * BANK], F32))

        def bank(n, k=1):
            return ps[:, n * BANK:(n + k) * BANK]

        COUNTS = bank(3)[:, 0:NB]

        off_in, idx_in, w_in, x_in = sem("off_in"), sem("idx_in"), sem("w_in"), sem("x_in")
        top_in = sem("top_in")
        consts_ready = sem("consts_ready")
        pool_step = sem("pool_step")
        dve_step = sem("dve_step")
        idx_ready = sem("idx_ready")
        thr_ready = sem("thr_ready")
        thr_turned = sem("thr_turned")
        digit_ready = sem("digit_ready")
        hot_ready = sem("hot_ready")
        counts_ready = sem("counts_ready")
        seg_ready = sem("seg_ready")
        kint_ready = sem("kint_ready")
        krow_in = sem("krow_in")
        slot_ready = sem("slot_ready")
        rows_in = [sem("rows_in_a"), sem("rows_in_b")]
        member_ready = sem("member_ready")
        member_used = sem("member_used")
        acc_read = sem("acc_read")
        turned = sem("turned")
        turned_read = sem("turned_read")
        mlp_made = sem("mlp_made")
        mlp_read = sem("mlp_read")
        pads_ready = sem("pads_ready")
        staged_ready = sem("staged_ready")
        gram_made = sem("gram_made")
        gram_act = sem("gram_act")
        gram_dve = sem("gram_dve")
        x_placed = sem("x_placed")
        top_made = sem("top_made")
        top_read = sem("top_read")
        out_done = [sem("out_done_a"), sem("out_done_b")]
        pool_held, dve_held, pe_held = sem("pool_held"), sem("dve_held"), sem("pe_held")

        block = ctx.enter_context(nc.Block())

        def stair_registers(engine_type, t):
            _, ks = nc.values_load_multi_w_load_instructions(
                k_row[0:1, bass.ds(t * 32, STEPS)], engines=(engine_type,), min_val=0, max_val=NB - 1,
                skip_runtime_bounds_check_because="k is a count of at most 15 blocks")
            return [nc.s_assert_within(k, max(0, s - NB + 1), min(NB - 1, s),
                                       skip_runtime_bounds_check_because="the staircase stays within the blocks")
                    for s, k in enumerate(ks)]

        def beat_steps(u):
            return range(4 * u, min(4 * u + 4, STEPS))

        def copy_unit(eng, copy, cs, done, unit):
            eng.wait_ge(gram_made, unit + 5)
            slot, par, col = (unit // UNITS) % 2, unit % 2, unit % UNITS * SUB * QUAD
            for c in cs:
                for m in range(QUAD):
                    n = len(range(1 + m, FEA, QUAD))
                    first = c * T + m
                    src = ps[32 * c:32 * c + 32, (4 + 2 * par) * BANK:(6 + 2 * par) * BANK].rearrange(
                        "p (h g j) -> p h g j", h=2, g=SUB)[:, :, :, first:first + (n - 1) * QUAD + 1:QUAD]
                    dst = z[32 * m:32 * m + 32, slot, 0:n, :, col + c:col + SUB * QUAD:QUAD]
                    last = copy(dst.rearrange("p n h g -> p h g n"), src)
            last.then_inc(done, 1)

        def stage_batch(batch):
            nc.vector.wait_ge(gram_made, 2 * batch + 2)
            by_bag = featT[:, :].rearrange("p (f b) -> p f b", f=FEA)
            nc.vector.tensor_copy(staged[:, batch % 2, :, 0:FEA],
                                  by_bag[:, :, batch * GB:(batch + 1) * GB].rearrange("p f b -> p b f")
                                  ).then_inc(staged_ready, 1)

        def gram_unit(unit):
            pe = nc.tensor
            if unit % 2 == 0:
                pe.wait_ge(staged_ready, unit // 2 + 1)
            pe.wait_ge(gram_act, unit + 1)
            pe.wait_ge(gram_dve, unit + 1)
            for g in range(SUB):
                for half in range(2):
                    b0 = SUB * QUAD * (unit % 2) + QUAD * g
                    four = staged[D * half:D * half + D, unit // 2 % 2, b0:b0 + QUAD, :]
                    at = (4 + 2 * (unit % 2) + half) * BANK + g * P
                    last = pe.matmul(ps[:, at:at + QUAD * T], four.rearrange("p b f -> p (b f)"),
                                     four[:, :, 1:FEA], start=True, stop=True)
            last.then_inc(gram_made, 1)

        FIRST_TILE_AT = (3, 6, 9, 12)
        TILE_AT = FIRST_TILE_AT + (13, 14, 15)

        @block.sync
        def _(sp):
            sp.dma_start(idx_raw, idx).then_inc(idx_in, 16)
            sp.dma_start(thr_raw, off).then_inc(off_in, 16)
            sp.dma_start(x_sb, xT).then_inc(x_in, 16)
            sp.dma_start(wb0, Wb0).then_inc(x_in, 16)
            sp.dma_start(wb1, Wb1.rearrange("(k p) n -> p k n", p=P)).then_inc(x_in, 16)
            sp.dma_start(wb2, Wb2.rearrange("(k p) n -> p k n", p=P)).then_inc(x_in, 16)
            for col, vec, n, w in ((cb0, bb0, H0, P), (cb1, bb1, H1, P), (cb2, bb2, D, D),
                                   (ct0, bt0, Y0, P), (ct1, bt1, Y1, P), (ct2, bt2, 1, 1)):
                sp.dma_start(bias[0:w, col:col + n // w], vec).then_inc(w_in, 16)
            sp.dma_start(wt2[:, :], Wt2).then_inc(w_in, 16)
            sp.dma_start(wt0[:, :, :], Wt0).then_inc(w_in, 16)
            sp.wait_ge(kint_ready, 1)
            sp.dma_start(k_row[0:1, :].rearrange("a (t s) -> a t s", t=T), k_int).then_inc(krow_in, 16)
            sp.wait_ge(turned_read, T + 1)
            sp.dma_start(wt1, Wt1.rearrange("(k p) n -> p k n", p=P)).then_inc(top_in, 16)
            answer = out.rearrange("a (h c b) -> a c h b", h=2, c=NCH)
            for c in range(NCH):
                sp.wait_ge(top_read, 7 * (c + 1))
                sp.dma_start(answer[:, c], y_out[0:1, (c % 2) * CH:(c % 2 + 1) * CH].rearrange(
                    "a (h b) -> a h b", h=2)).then_inc(out_done[c % 2], 16)
            sp.wait_ge(out_done[0], 16 * NCH // 2)
            sp.wait_ge(out_done[1], 16 * NCH // 2)

        W_IN = 8 * 16

        @block.gpsimd
        def _(pool):
            g = nc.gpsimd
            small = dict(channel_multiplier=0, allow_small_or_imprecise_dtypes=True)
            g.iota(idx_base, [[ROWS, T], [0, NB]], base=0, channel_multiplier=0).then_inc(consts_ready, 1)
            g.memset(ident[:, :], 0.0).then_inc(pool_step, 1)
            pool.wait_ge(pool_step, 1)
            g.affine_select(out=ident[:, :], in_=ident[:, :], compare_op=ALU.not_equal, fill=1.0, base=0,
                            pattern=[[-1, P]], channel_multiplier=1).then_inc(consts_ready, 1)
            g.iota(block_end, [[P, NB]], base=P, **small).then_inc(consts_ready, 1)
            g.iota(iota_l[:, :], [[1, P]], base=0, **small).then_inc(consts_ready, 1)
            g.iota(iota_h[:, :], [[1, NB]], base=0, **small).then_inc(consts_ready, 1)
            g.iota(bag_base[:, :], [[P, NB]], base=0, **small).then_inc(consts_ready, 1)
            g.memset(ones[:, :], 1.0).then_inc(consts_ready, 1)
            g.memset(zeros[:, :], 0.0).then_inc(consts_ready, 1)
            g.memset(staged[:, :, :, :], 0.0).then_inc(pads_ready, 1)
            table_rows = tables.rearrange("t r d -> (t r) d")
            with pool.Fori(0, T // 2) as it:
                for par in range(2):
                    pool.wait_ge(slot_ready, 2 * it + par + 1)
                    pool.sem_inc(pool_held, 1)
                    for k in range(NB):
                        g.indirect_dma_start(
                            rows[:, par, k * D:(k + 1) * D], None, table_rows,
                            bass.IndirectOffsetOnAxis(ap=idx_slot[:, par, k:k + 1], axis=0),
                        ).then_inc(rows_in[par], 16)

        CONSTS = 8

        @block.vector
        def _(dve):
            v = nc.vector
            chain = [0]

            def link(ins):
                chain[0] += 1
                ins.then_inc(dve_step, 1)
                dve.wait_ge(dve_step, chain[0])

            dve.wait_ge(idx_in, 16)
            dve.wait_ge(consts_ready, 1)
            v.memset(idx_all[:, TN:], 0)
            v.tensor_tensor(idx_all[:, 0:TN], idx_raw, idx_base, ALU.add).then_inc(idx_ready, 1)

            dve.wait_ge(off_in, 16)
            v.memset(lo_all[:, TN:], 0.0)
            v.memset(hi_all[:, TN:], 0.0)
            v.memset(thr[:, 0:1], 0.0)
            v.memset(thr[:, B:B + 1], float(B))
            v.tensor_copy(off0, thr_raw[:, 0:1])
            link(v.tensor_copy(thr[:, 1:B], thr_raw[:, 1:B]))
            s = B // 2
            while s:
                n = B // (2 * s)
                mid = thr[:, s:s + (n - 1) * 2 * s + 1:2 * s]
                left = thr[:, 0:(n - 1) * 2 * s + 1:2 * s]
                right = thr[:, 2 * s:2 * s + (n - 1) * 2 * s + 1:2 * s]
                link(v.tensor_tensor(mid, mid, left, ALU.max))
                link(v.tensor_tensor(mid, mid, right, ALU.min))
                s //= 2
            link(v.tensor_scalar(off0, off0, 0.0, None, ALU.max))
            v.tensor_tensor(thr[:, 0:1], off0, thr[:, 1:2], ALU.min).then_inc(thr_ready, 1)

            dve.wait_ge(consts_ready, CONSTS)
            table = passed.rearrange("p (k j) -> p k j", k=NB - 1)
            v.memset(table[:, :, 0:LAG + 1], 0.0)
            v.memset(table[:, :, LAG + NB:], 1.0)
            starts = thr[:, P:B:P].rearrange("p (k j) -> p k j", k=1).broadcast_to([T, NB - 1, NB - 1])
            ends = block_end[0:T, 0:NB - 1].rearrange("p (k j) -> p k j", j=1).broadcast_to([T, NB - 1, NB - 1])
            link(v.tensor_tensor(table[:, :, LAG + 1:LAG + NB], starts, ends, ALU.is_ge))
            diagonal = passed[:, LAG:LAG + (NB - 1) * (PW - 1)].rearrange("p (k s) -> p s k", k=NB - 1)
            v.memset(k_int, 0)
            link(v.tensor_reduce(k_of_step[:, 0:STEPS], diagonal[:, 0:STEPS, :], AX.X, ALU.add))
            v.tensor_copy(k_int[:, 0:STEPS], k_of_step[:, 0:STEPS]).then_inc(kint_ready, 1)

            dve.wait_ge(thr_turned, 1)
            link(v.tensor_copy(thr_i.rearrange("p (t c) -> p c t", t=T),
                               bank(0)[:, 0:TN].rearrange("p (c t) -> p c t", t=T)))
            link(v.tensor_scalar(lo_i, thr_i, P - 1, None, ALU.bitwise_and))
            link(v.tensor_scalar(hi_i, thr_i, 7, None, ALU.arith_shift_right))
            link(v.tensor_copy(lo_all[:, 0:TN], lo_i))
            link(v.tensor_copy(hi_all[:, 0:TN], hi_i))

            def digits(t):
                hi = hi_all[:, bass.ds(t * NB, NB)].rearrange("p (c h) -> p c h", h=1).broadcast_to([P, NB, NB])
                io = iota_h[:, :].rearrange("p (c h) -> p c h", c=1).broadcast_to([P, NB, NB])
                v.tensor_tensor(eq_hi[:, :, :], hi, io, ALU.is_equal)
                v.tensor_tensor(lt_hi[:, :, :], hi, io, ALU.is_lt)
                v.tensor_copy(lo_slot[:, :], lo_all[:, bass.ds(t * NB, NB)]).then_inc(digit_ready, 1)
                dve.wait_ge(digit_ready, t + 1)
                dve.sem_inc(dve_held, 1)

            def low_digit(c):
                return v.tensor_scalar(ge_lo[:, c, :], iota_l[:, :], lo_slot[:, c:c + 1], None, ALU.is_ge)

            def find_seg(par, t):
                dve.wait_ge(counts_ready, t + 1)
                v.tensor_scalar(seg[:, par, :], COUNTS, -1.0, None, ALU.add).then_inc(seg_ready, 1)

            digits(0)
            for c in range(NB):
                last = low_digit(c)
            last.then_inc(hot_ready, 1)
            find_seg(0, 0)

            def table_sums(par, t):
                ks = stair_registers(mybir.EngineType.DVE, t)
                dve.wait_ge(seg_ready, t + 1)
                dve.sem_inc(dve_held, 1)
                for u in range(BEATS):
                    s1 = beat_steps(u)[-1]
                    seen = STEPS * t + STEPS + (s1 - 16) + 1 if s1 >= 16 else STEPS * t + min(s1 + 16, STEPS - 1) + 1
                    dve.wait_ge(member_used, seen)
                    dve.sem_inc(dve_held, 1)
                    for s in beat_steps(u):
                        v.tensor_scalar(member[:, s % 16, :], iota_l[:, :], bag_base[:, bass.ds(s - ks[s], 1)],
                                        seg[:, par, bass.ds(ks[s], 1)], ALU.add,
                                        ALU.is_equal).then_inc(member_ready, 1)
                    if u == 0:
                        digits(t + 1)
                    for c in (2 * u, 2 * u + 1):
                        last = low_digit(c)
                    if u == BEATS - 1:
                        last.then_inc(hot_ready, 1)
                find_seg(1 - par, t + 1)

            dve.wait_ge(krow_in, 16)
            with dve.Fori(0, T // 2) as it:
                for par in range(2):
                    table_sums(par, 2 * it + par)

            dve.wait_ge(pads_ready, 1)
            dve.wait_ge(turned_read, T + 1)
            stage_batch(0)
            for unit in range(NCH * UNITS):
                if unit % 2 == 0 and unit + 2 < NCH * UNITS:
                    stage_batch(unit // 2 + 1)
                if unit % UNITS == 0 and unit >= 2 * UNITS:
                    dve.wait_ge(top_made, 7 * (unit // UNITS - 2) + 4)
                copy_unit(dve, v.tensor_copy, (3,), gram_dve, unit)

        @block.scalar
        def _(act):
            a = nc.scalar

            def hand_indices(par, t):
                a.copy(idx_slot[:, par, :], idx_all[:, bass.ds(t * NB, NB)]).then_inc(slot_ready, 1)

            def mlp_chunk(c, half):
                n = c + (2 * half)
                for i in range(7):
                    act.wait_ge(mlp_made, 7 * n + i + 1)
                    src = bank(6 + i % 2)
                    if i < 4:
                        a.activation(hid0[:, i, :], src, ACT.Relu, bias=bias[:, cb0 + i:cb0 + i + 1]).then_inc(mlp_read, 1)
                    elif i < 6:
                        a.activation(hid1[:, i - 4, :], src, ACT.Relu,
                                     bias=bias[:, cb1 + i - 4:cb1 + i - 3]).then_inc(mlp_read, 1)
                    else:
                        a.activation(featT[D * half:D * half + D, bass.ds(c * CH, CH)], src[0:D, :],
                                     ACT.Relu, bias=bias[0:D, cb2:cb2 + 1]).then_inc(mlp_read, 1)

            def table(par, t):
                act.wait_ge(member_used, t * STEPS + 2 * STEPS)
                a.copy(pooled.rearrange("p (j h d) -> p h j d", h=2, d=D),
                       bank(0, 2).rearrange("p (h j d) -> p h j d", h=2, d=D)).then_inc(acc_read, 1)
                hand_indices(par, t + 2)
                act.wait_ge(turned, t + 1)
                a.copy(featT[:, bass.ds((t + 1) * HALF, HALF)], bank(0, 2)).then_inc(turned_read, 1)

            act.wait_ge(idx_ready, 1)
            hand_indices(0, 0)
            hand_indices(1, 1)
            act.wait_ge(w_in, W_IN)
            act.wait_ge(thr_turned, 1)
            for half in range(2):
                with act.Fori(0, 2) as c:
                    mlp_chunk(c, half)
                    for par in range(2):
                        table(par, 4 * half + 2 * c + par)
            with act.Fori(4, T // 2) as it:
                for par in range(2):
                    table(par, 2 * it + par)

            def top_tile(c, i):
                act.wait_ge(top_made, 7 * c + i + 1)
                if i < 4:
                    a.activation(top0[:, i, :], bank(i), ACT.Relu, bias=bias[:, ct0 + i:ct0 + i + 1]).then_inc(top_read, 1)
                elif i < 6:
                    a.activation(top1[:, i - 4, :], bank(i - 4), ACT.Relu,
                                 bias=bias[:, ct1 + i - 4:ct1 + i - 3]).then_inc(top_read, 1)
                else:
                    if c >= 2:
                        act.wait_ge(out_done[c % 2], 16 * (c // 2))
                    a.activation(y_out[0:1, (c % 2) * CH:(c % 2 + 1) * CH], bank(2)[0:1, :], ACT.Sigmoid,
                                 bias=bias[0:1, ct2:ct2 + 1]).then_inc(top_read, 1)

            for c in range(NCH):
                if c >= 2:
                    act.wait_ge(top_made, 7 * (c - 2) + 4)
                for half in range(2):
                    last = a.copy(z[D:P, c % 2, NJ - 1, half, :],
                                  featT[D * half:D * half + D, c * HCH:(c + 1) * HCH])
                last.then_inc(x_placed, 1)
                for u in range(UNITS):
                    copy_unit(act, a.copy, (0, 1, 2), gram_act, UNITS * c + u)
                    if c and u in TILE_AT:
                        top_tile(c - 1, TILE_AT.index(u))
            for i in range(7):
                top_tile(NCH - 1, i)

        @block.tensor
        def _(pe):
            mm = nc.tensor.matmul
            pe.sem_inc(member_used, STEPS)
            pe.sem_inc(turned_read, 1)
            pe.sem_inc(mlp_read, 1)
            pe.sem_inc(gram_made, 4)
            pe.sem_inc(gram_act, 2)
            pe.sem_inc(gram_dve, 2)

            pe.wait_ge(consts_ready, CONSTS)
            pe.wait_ge(thr_ready, 1)
            for c in range(NB):
                last = nc.tensor.transpose(bank(0)[:, c * T:(c + 1) * T], thr[:, c * P:(c + 1) * P], ident[0:T, 0:T])
            last.then_inc(thr_turned, 1)

            def count(t):
                pe.wait_ge(hot_ready, t + 1)
                for c in range(NB):
                    mm(COUNTS, ones[:, :], lt_hi[:, c, :], start=(c == 0), stop=False)
                for c in range(NB):
                    last = mm(COUNTS, ge_lo[:, c, :], eq_hi[:, c, :], start=False, stop=(c == NB - 1))
                last.then_inc(counts_ready, 1)

            count(0)

            def top_products(c, i):
                zc = z[:, c % 2].rearrange("p n h b -> p n (h b)")
                if i < 4:
                    ops = [(bank(i), wt0[:, n, i * P:(i + 1) * P], zc[:, n]) for n in range(NJ)]
                elif i < 6:
                    ops = [(bank(i - 4), wt1[:, k, (i - 4) * P:(i - 3) * P], top0[:, k, :]) for k in range(Y0 // P)]
                else:
                    ops = [(bank(2)[0:1, :], wt2[:, k:k + 1], top1[:, k, :]) for k in range(Y1 // P)]
                return ops

            def top_tile(c, i, part=0, of=1):
                ops = top_products(c, i)
                if part == 0:
                    if i == 0:
                        pe.wait_ge(x_placed, c + 1)
                        pe.wait_ge(gram_act, UNITS * (c + 1) + 2)
                        pe.wait_ge(gram_dve, UNITS * (c + 1) + 2)
                        if c == 0:
                            pe.wait_ge(top_in, 16)
                    if i < 4:
                        if c:
                            pe.wait_ge(top_read, 7 * (c - 1) + (5, 6, 7, 4)[i])
                    else:
                        pe.wait_ge(top_read, 7 * c + (4, 4, 6)[i - 4])
                for k in range(len(ops) * part // of, len(ops) * (part + 1) // of):
                    dst, weights, moving = ops[k]
                    last = mm(dst, weights, moving, start=(k == 0), stop=(k == len(ops) - 1))
                if part == of - 1:
                    last.then_inc(top_made, 1)

            def mlp_chunk(c, half):
                n7 = 7 * c + 14 * half
                for i in range(7):
                    pe.wait_ge(mlp_read, n7 + (1, 1, 2, 3, 5, 5, 7)[i])
                    if i < 4:
                        pe.sem_inc(pe_held, 1)
                    dst = bank(6 + i % 2)
                    if i < 4:
                        mm(dst, wb0[:, i * P:(i + 1) * P], x_sb[:, bass.ds(half * HALF + c * CH, CH)],
                           start=True, stop=True).then_inc(mlp_made, 1)
                    elif i < 6:
                        for k in range(H0 // P):
                            last = mm(dst, wb1[:, k, (i - 4) * P:(i - 3) * P], hid0[:, k, :],
                                      start=(k == 0), stop=(k == H0 // P - 1))
                        last.then_inc(mlp_made, 1)
                    else:
                        for k in range(H1 // P):
                            last = mm(dst[0:D, :], wb2[:, k, :], hid1[:, k, :], start=(k == 0), stop=(k == H1 // P - 1))
                        last.then_inc(mlp_made, 1)

            def table(par, it, t):
                ks = stair_registers(mybir.EngineType.PE, t)
                pe.wait_ge(turned_read, t + 1)
                for h in range(2):
                    mm(bank(h)[:, 0:D], zeros[:, :], zeros[:, 0:D], start=True, stop=False, skip_group_check=True)
                pe.wait_ge(rows_in[par], 256 * it + 256)
                for u in range(BEATS):
                    for s in beat_steps(u):
                        pe.wait_ge(member_ready, t * STEPS + s + 1)
                        mm(ps[:, bass.ds((s - ks[s]) * D, D)], member[:, s % 16, :],
                           rows[:, par, bass.ds(ks[s] * D, D)], start=False, stop=(s == STEPS - 1),
                           skip_group_check=True).then_inc(member_used, 1)
                count(t + 1)
                pe.wait_ge(acc_read, t + 1)
                for j in range(NB // 2):
                    last = nc.tensor.transpose(bank(0, 2)[:, j * P:(j + 1) * P], pooled[:, j * P:(j + 1) * P], ident[:, :])
                last.then_inc(turned, 1)

            pe.wait_ge(krow_in, 16)
            pe.wait_ge(x_in, 64)
            pe.wait_ge(w_in, W_IN)
            for half in range(2):
                with pe.Fori(0, 2) as c:
                    mlp_chunk(c, half)
                    for par in range(2):
                        table(par, 2 * half + c, 4 * half + 2 * c + par)
            with pe.Fori(4, T // 2) as it:
                for par in range(2):
                    table(par, it, 2 * it + par)

            for c in range(NCH):
                for u in range(UNITS):
                    gram_unit(UNITS * c + u)
                    if c and 1 <= u <= 12:
                        top_tile(c - 1, (u - 1) // 3, (u - 1) % 3, 3)
                    elif c and u > 12:
                        top_tile(c - 1, u - 9)
            for i in range(7):
                top_tile(NCH - 1, i)


_INS = ["off", "idx", "tables", "xT", "Wb0", "bb0", "Wb1", "bb1", "Wb2", "bb2", "Wt0", "bt0", "Wt1", "bt1", "Wt2", "bt2"]


def kernel(r_dense_x, r_sparse_off, L0_rec_sparse_idx, L0_rec_emb_tables, L0_rec_W_bot0, L0_rec_b_bot0,
           L0_rec_W_bot1, L0_rec_b_bot1, L0_rec_W_bot2, L0_rec_b_bot2, L0_rec_W_top0, L0_rec_b_top0,
           L0_rec_W_top1, L0_rec_b_top1, L0_rec_W_top2, L0_rec_b_top2):
    import numpy as np
    import concourse.bacc as bacc
    from concourse.bass_utils import run_bass_kernel_spmd as run

    def column(vec, w):
        return np.ascontiguousarray(np.asarray(vec).reshape(-1, w).T)

    w0 = np.asarray(L0_rec_W_top0)
    wt0 = np.zeros((P, NJ, Y0), w0.dtype)
    row = D
    for i in range(FEA):
        for j in range(i + 1, FEA):
            wt0[32 * ((j - 1) % QUAD) + i, (j - 1) // QUAD] = w0[row]
            row += 1
    wt0[D:P, NJ - 1] = w0[0:D]
    data = {
        "off": np.asarray(r_sparse_off),
        "idx": np.ascontiguousarray(np.asarray(L0_rec_sparse_idx).reshape(T, NB, P).transpose(2, 0, 1).reshape(P, T * NB)),
        "tables": np.asarray(L0_rec_emb_tables),
        "xT": np.ascontiguousarray(np.asarray(r_dense_x).T),
        "Wb0": np.asarray(L0_rec_W_bot0), "bb0": column(L0_rec_b_bot0, P),
        "Wb1": np.asarray(L0_rec_W_bot1), "bb1": column(L0_rec_b_bot1, P),
        "Wb2": np.asarray(L0_rec_W_bot2), "bb2": column(L0_rec_b_bot2, D),
        "Wt0": wt0, "bt0": column(L0_rec_b_top0, P),
        "Wt1": np.asarray(L0_rec_W_top1), "bt1": column(L0_rec_b_top1, P),
        "Wt2": column(L0_rec_W_top2, P), "bt2": column(L0_rec_b_top2, 1),
    }
    nc = bacc.Bacc("TRN2", target_bir_lowering=False, num_devices=1)
    args = [nc.dram_tensor(n, data[n].shape, mybir.dt.from_np(data[n].dtype), kind="ExternalInput").ap() for n in _INS]
    out = nc.dram_tensor("out", (1, B), F32, kind="ExternalOutput").ap()
    build(nc, *args, out)
    result = run(nc, [data], core_ids=[0])
    return result.results[0]["out"].reshape(B)
```

```python
from contextlib import ExitStack

import concourse.bass as bass
from concourse import mybir

F32 = mybir.dt.float32
BF16 = mybir.dt.bfloat16
F16 = mybir.dt.float16
I32 = mybir.dt.int32
ALU = mybir.AluOpType
ACT = mybir.ActivationFunctionType
AX = mybir.AxisListType

P = 128
T = 26
FEA = T + 1
ROWS = 12500
D = 64
B = 2048
NB = B // P
HALF = B // 2
STEPS = 2 * NB - 1
DENSE, H0, H1 = 13, 512, 256
Y0, Y1 = 512, 256
CH = 256
NCH = B // CH
HCH = CH // 2
QUAD = 4
FPAD = 32
PAD = FPAD - FEA
NJ = (T - PAD + QUAD - 1) // QUAD
SUB = 4
UNITS = HCH // (SUB * QUAD)
GB = 2 * SUB * QUAD
BANK = 512
BEATS = 8
ROWS_LEFT = NB + NB // 2 - 1
LAG = NB - 2


def build(nc, off, idx, tables, xT, Wb0, bb0, Wb1, bb1, Wb2, bb2, Wt0, bt0, Wt1, bt1, Wt2, bt2, out):
    with ExitStack() as ctx:
        def sb(name, shape, dt=F32):
            return ctx.enter_context(nc.sbuf_tensor(name, shape, dt))

        def sem(name):
            return ctx.enter_context(nc.semaphore(name))

        featT = sb("featT", [P, FEA * HALF])
        wt0 = sb("wt0", [P, NJ, Y0])
        z = sb("z", [P, 2, NJ, 2, HCH])
        x_sb = sb("x_sb", [DENSE, B])
        hid1 = sb("hid1", [P, H1 // P, CH])
        still = sb("still", [P, 2, GB, FPAD])
        moving = sb("moving", [P, 2, GB // QUAD, 2, QUAD, T])
        NR = NB * D
        loop = sb("loop", [P, 2 * NR + 16 * P + NR])
        ge_lo = sb("ge_lo", [P, NB, P], BF16)
        eq_hi = sb("eq_hi", [P, NB, NB], BF16)
        lt_hi = sb("lt_hi", [P, NB, NB], BF16)
        lo_all = sb("lo_all", [P, (T + 1) * NB], F16)
        hi_all = sb("hi_all", [P, (T + 1) * NB], F16)
        lo_slot = sb("lo_slot", [P, NB])
        idx_all = sb("idx_all", [P, (T + 2) * NB], I32)
        idx_slot = sb("idx_slot", [P, 2, NB], I32)
        seg = sb("seg", [P, 2, NB])
        k_row = sb("k_row", [1, T * 32], I32)
        ident = sb("ident", [P, P])
        iota_l = sb("iota_l", [P, P], BF16)
        ones = sb("ones", [P, P], BF16)
        zeros = sb("zeros", [P, P], BF16)
        iota_h = sb("iota_h", [P, NB])
        bag_base = sb("bag_base", [P, NB])
        wt2 = sb("wt2", [P, Y1 // P])
        bias = sb("bias", [P, 16])
        cb0, cb1, cb2, ct0, ct1, ct2 = 0, 4, 6, 7, 11, 13

        def parts(tile, *widths):
            at, found = 0, []
            for w in widths:
                found.append(tile[:, at:at + w])
                at += w
            return found

        rows, member, pooled = parts(loop, 2 * NR, 16 * P, NR)
        rows = rows.rearrange("p (a r) -> p a r", a=2)
        member = member.rearrange("p (s b) -> p s b", b=P)
        top0, top1, wt1, y_out = parts(loop, Y0 // P * CH, Y1 // P * CH, Y0 // P * Y1, 2 * CH)
        top0 = top0.rearrange("p (m c) -> p m c", c=CH)
        top1 = top1.rearrange("p (m c) -> p m c", c=CH)
        wt1 = wt1.rearrange("p (k n) -> p k n", n=Y1)
        early = z[:, :, :, :, :].rearrange("p s n h b -> p (s n h b)")
        wb0, wb1, wb2, hid0 = parts(early, H0, H0 // P * H1, H1 // P * D, H0 // P * CH)
        wb1 = wb1.rearrange("p (k n) -> p k n", n=H1)
        wb2 = wb2.rearrange("p (k n) -> p k n", n=D)
        hid0 = hid0.rearrange("p (m c) -> p m c", c=CH)
        wb0 = wb0[0:DENSE, :]
        late = featT[:, (FEA - 8) * HALF:]
        TN = T * NB
        PW = STEPS + LAG
        (thr_raw, thr_i, lo_i, hi_i, idx_raw, idx_base, passed, block_end, k_of_step, k_int, off0, thr) = parts(
            late, B, TN, TN, TN, TN, TN, (NB - 1) * PW, NB, 32, 32, 1, B + 1)
        thr_raw, thr_i, lo_i, hi_i, idx_raw, idx_base, k_int = (
            x.bitcast(I32) for x in (thr_raw, thr_i, lo_i, hi_i, idx_raw, idx_base, k_int))
        thr_raw, passed, k_of_step, k_int, off0, thr = (
            x[0:T, :] for x in (thr_raw, passed, k_of_step, k_int, off0, thr))

        ps = ctx.enter_context(nc.psum_tensor("ps", [P, 8 * BANK], F32))

        def bank(n, k=1):
            return ps[:, n * BANK:(n + k) * BANK]

        COUNTS = bank(3)[:, 0:NB]
        ACC = (0, 4)

        off_in, idx_in, w_in, x_in = sem("off_in"), sem("idx_in"), sem("w_in"), sem("x_in")
        top_in = sem("top_in")
        consts_ready = sem("consts_ready")
        pool_step = sem("pool_step")
        dve_step = sem("dve_step")
        idx_ready = sem("idx_ready")
        thr_ready = sem("thr_ready")
        thr_turned = sem("thr_turned")
        digit_ready = sem("digit_ready")
        hot_ready = sem("hot_ready")
        counts_ready = sem("counts_ready")
        seg_ready = sem("seg_ready")
        kint_ready = sem("kint_ready")
        krow_in = sem("krow_in")
        slot_ready = sem("slot_ready")
        rows_in = [[sem(f"rows_in_{par}{h}") for h in "ab"] for par in ("even_", "odd_")]
        member_ready = sem("member_ready")
        member_used = sem("member_used")
        acc_read = sem("acc_read")
        turned = sem("turned")
        turned_read = sem("turned_read")
        mlp_made = sem("mlp_made")
        mlp_read = sem("mlp_read")
        zeros_ready = sem("zeros_ready")
        staged = sem("staged")
        gram_made = sem("gram_made")
        gram_act = sem("gram_act")
        gram_dve = sem("gram_dve")
        spare_act = sem("spare_act")
        spare_dve = sem("spare_dve")
        x_placed = sem("x_placed")
        top_made = sem("top_made")
        top_read = sem("top_read")
        out_done = [sem("out_done_a"), sem("out_done_b")]
        pool_held, dve_held, pe_held = sem("pool_held"), sem("dve_held"), sem("pe_held")

        block = ctx.enter_context(nc.Block())

        def stair_registers(engine_type, t):
            _, ks = nc.values_load_multi_w_load_instructions(
                k_row[0:1, bass.ds(t * 32, STEPS)], engines=(engine_type,), min_val=0, max_val=NB - 1,
                skip_runtime_bounds_check_because="k is a count of at most 15 blocks")
            return [nc.s_assert_within(k, max(0, s - NB + 1), min(NB - 1, s),
                                       skip_runtime_bounds_check_because="the staircase stays within the blocks")
                    for s, k in enumerate(ks)]

        def beat_steps(u):
            return range(4 * u, min(4 * u + 4, STEPS))

        def each_chunk(engine, do):
            do(0, 0, True, False)
            with engine.Fori(0, NCH // 2 - 1) as i:
                do(2 * i + 1, 1, False, False)
                do(2 * i + 2, 0, False, False)
            do(NCH - 1, 1, False, True)

        def copy_unit(eng, copy, cs, spare, done, c, slot, u):
            unit, par, col = UNITS * c + u, u % 2, u * SUB * QUAD
            eng.wait_ge(gram_made, unit + 5)
            banks = ps[:, (4 + 2 * par) * BANK:(6 + 2 * par) * BANK].rearrange("p (g h j) -> p h g j", h=2, g=SUB)

            def z_of(bag):
                return z[:, slot, :, :, col + bag:col + SUB * QUAD:QUAD].rearrange("p n h g -> p h g n")

            for bag in cs:
                last = copy(z_of(bag)[0:FPAD], banks[32 * bag:32 * bag + 32, :, :, bag * T:bag * T + NJ])
            last.then_inc(spare, 1)
            for m in (1, 2, 3, 0):
                if m == 0:
                    eng.wait_ge(spare, unit + 1)
                r = FPAD if m else FEA
                n = len(range(1 + PAD + m, FEA, QUAD))
                for bag in cs:
                    first = bag * T + PAD + m
                    last = copy(z_of(bag)[32 * m:32 * m + r, :, :, 0:n],
                                banks[32 * bag:32 * bag + r, :, :, first:first + (n - 1) * QUAD + 1:QUAD])
            last.then_inc(done, 1)

        def bags_of(at, rows_of, first, end):
            return featT[rows_of, first * HALF:end * HALF].rearrange("p (f b) -> p b f", b=HALF)[
                :, bass.ds(at, GB)]

        def stage_still(copy, at, slot, first, end):
            copy(still[:, slot, :, first:end], bags_of(at, slice(0, P), first, end))
            if first == 0:
                copy(still[:, slot, :, FEA:], bags_of(at, slice(0, P), 0, PAD))

        def stage_moving(copy, at, slot, half, first, end):
            first = max(first, 1)
            rows_of = slice(D * half, D * half + D)
            return copy(moving[rows_of, slot, :, half, :, first - 1:end - 1],
                        bags_of(at, rows_of, first, end).rearrange("p (g b) f -> p g b f", b=QUAD))

        def gram_unit(c, u):
            pe, unit = nc.tensor, UNITS * c + u
            if u % 2 == 0:
                pe.wait_ge(staged, UNITS // 2 * c + (u // 2 + 1))
            pe.wait_ge(gram_act, unit + 1)
            pe.wait_ge(gram_dve, unit + 1)
            slot = u // 2 % 2
            for g in range(SUB):
                group = SUB * (u % 2) + g
                at = (4 + 2 * (u % 2)) * BANK + 2 * P * g
                last = pe.matmul(ps[:, at:at + 2 * P].rearrange("p (h j) -> p h j", h=2)[:, :, 0:QUAD * T],
                                 still[:, slot, QUAD * group:QUAD * (group + 1)].rearrange("p b f -> p (b f)"),
                                 moving[:, slot, group].rearrange("p h b f -> p h (b f)"), start=True, stop=True)
            last.then_inc(gram_made, 1)

        MLP_FROM = T // 2 - NCH
        MLP_TILES = {0: [0], 2: [1], 4: [2], 6: [3]}, {0: [4], 2: [5], 4: [6]}
        LAST_TILES = MLP_TILES[0], {1: [4]}


        @block.sync
        def _(sp):
            sp.dma_start(idx_raw, idx).then_inc(idx_in, 16)
            sp.dma_start(thr_raw, off).then_inc(off_in, 16)
            sp.dma_start(x_sb[:, :], xT).then_inc(x_in, 16)
            sp.dma_start(wb0, Wb0).then_inc(x_in, 16)
            sp.dma_start(wb1, Wb1.rearrange("(k p) n -> p k n", p=P)).then_inc(x_in, 16)
            sp.dma_start(wb2, Wb2.rearrange("(k p) n -> p k n", p=P)).then_inc(x_in, 16)
            for col, vec, n, w in ((cb0, bb0, H0, P), (cb1, bb1, H1, P), (cb2, bb2, D, D),
                                   (ct0, bt0, Y0, P), (ct1, bt1, Y1, P), (ct2, bt2, 1, 1)):
                sp.dma_start(bias[0:w, col:col + n // w], vec).then_inc(w_in, 16)
            sp.dma_start(wt2[:, :], Wt2).then_inc(w_in, 16)
            sp.dma_start(wt0[:, :, :], Wt0).then_inc(w_in, 16)
            sp.wait_ge(kint_ready, 1)
            sp.dma_start(k_row[0:1, :].rearrange("a (t s) -> a t s", t=T), k_int).then_inc(krow_in, 16)
            sp.wait_ge(turned_read, T + 2)
            sp.dma_start(wt1, Wt1.rearrange("(k p) n -> p k n", p=P)).then_inc(top_in, 16)
            answer = out.rearrange("a (h c b) -> a c h b", h=2, c=NCH)
            for c in range(NCH):
                sp.wait_ge(top_read, 7 * (c + 2))
                sp.dma_start(answer[:, c], y_out[0:1, (c % 2) * CH:(c % 2 + 1) * CH].rearrange(
                    "a (h b) -> a h b", h=2)).then_inc(out_done[c % 2], 16)
            for done in out_done:
                sp.wait_ge(done, 16 + 16 * NCH // 2)

        W_IN = 8 * 16

        @block.gpsimd
        def _(pool):
            g = nc.gpsimd
            small = dict(channel_multiplier=0, allow_small_or_imprecise_dtypes=True)
            g.iota(idx_base, [[ROWS, T], [0, NB]], base=0, channel_multiplier=0).then_inc(consts_ready, 1)
            g.memset(ident[:, :], 0.0).then_inc(pool_step, 1)
            pool.wait_ge(pool_step, 1)
            g.affine_select(out=ident[:, :], in_=ident[:, :], compare_op=ALU.not_equal, fill=1.0, base=0,
                            pattern=[[-1, P]], channel_multiplier=1).then_inc(consts_ready, 1)
            g.iota(block_end, [[P, NB]], base=P, **small).then_inc(consts_ready, 1)
            g.iota(iota_l[:, :], [[1, P]], base=0, **small).then_inc(consts_ready, 1)
            g.iota(iota_h[:, :], [[1, NB]], base=0, **small).then_inc(consts_ready, 1)
            g.iota(bag_base[:, :], [[P, NB]], base=0, **small).then_inc(consts_ready, 1)
            g.memset(ones[:, :], 1.0).then_inc(consts_ready, 1)
            g.memset(zeros[:, :], 0.0).then_inc(consts_ready, 1)
            table_rows = tables.rearrange("t r d -> (t r) d")
            with pool.Fori(0, T // 2) as it:
                for par in range(2):
                    for h in range(2):
                        pool.wait_ge(slot_ready, 4 * it + 2 * par + h + 1)
                        pool.sem_inc(pool_held, 1)
                        for k in range(h * NB // 2, (h + 1) * NB // 2):
                            g.indirect_dma_start(
                                rows[:, par, k * D:(k + 1) * D], None, table_rows,
                                bass.IndirectOffsetOnAxis(ap=idx_slot[:, par, k:k + 1], axis=0),
                            ).then_inc(rows_in[par][h], 16)

            g.memset(moving[0:D, :, :, 1], 0.0).then_inc(pool_step, 1)
            g.memset(moving[D:P, :, :, 0], 0.0).then_inc(pool_step, 1)
            pool.wait_ge(pool_step, 3)
            pool.sem_inc(zeros_ready, 1)
            pool.wait_ge(mlp_read, 7 * NCH + 1)
            g.memset(z[32:D, :, NJ - 1], 0.0).then_inc(zeros_ready, 1)

        CONSTS = 8

        @block.vector
        def _(dve):
            v = nc.vector
            chain = [0]

            def link(ins):
                chain[0] += 1
                ins.then_inc(dve_step, 1)
                dve.wait_ge(dve_step, chain[0])

            dve.wait_ge(idx_in, 16)
            dve.wait_ge(consts_ready, 1)
            v.memset(idx_all[:, TN:], 0)
            v.tensor_tensor(idx_all[:, 0:TN], idx_raw, idx_base, ALU.add).then_inc(idx_ready, 1)

            v.memset(pooled, 0.0).then_inc(acc_read, 1)

            dve.wait_ge(off_in, 16)
            v.memset(lo_all[:, TN:], 0.0)
            v.memset(hi_all[:, TN:], 0.0)
            v.memset(thr[:, 0:1], 0.0)
            v.memset(thr[:, B:B + 1], float(B))
            v.tensor_copy(off0, thr_raw[:, 0:1])
            link(v.tensor_copy(thr[:, 1:B], thr_raw[:, 1:B]))
            s = B // 2
            while s:
                n = B // (2 * s)
                mid = thr[:, s:s + (n - 1) * 2 * s + 1:2 * s]
                left = thr[:, 0:(n - 1) * 2 * s + 1:2 * s]
                right = thr[:, 2 * s:2 * s + (n - 1) * 2 * s + 1:2 * s]
                link(v.tensor_tensor(mid, mid, left, ALU.max))
                link(v.tensor_tensor(mid, mid, right, ALU.min))
                s //= 2
            link(v.tensor_scalar(off0, off0, 0.0, None, ALU.max))
            v.tensor_tensor(thr[:, 0:1], off0, thr[:, 1:2], ALU.min).then_inc(thr_ready, 1)

            dve.wait_ge(consts_ready, CONSTS)
            table = passed.rearrange("p (k j) -> p k j", k=NB - 1)
            v.memset(table[:, :, 0:LAG + 1], 0.0)
            v.memset(table[:, :, LAG + NB:], 1.0)
            starts = thr[:, P:B:P].rearrange("p (k j) -> p k j", k=1).broadcast_to([T, NB - 1, NB - 1])
            ends = block_end[0:T, 0:NB - 1].rearrange("p (k j) -> p k j", j=1).broadcast_to([T, NB - 1, NB - 1])
            link(v.tensor_tensor(table[:, :, LAG + 1:LAG + NB], starts, ends, ALU.is_ge))
            diagonal = passed[:, LAG:LAG + (NB - 1) * (PW - 1)].rearrange("p (k s) -> p s k", k=NB - 1)
            v.memset(k_int, 0)
            link(v.tensor_reduce(k_of_step[:, 0:STEPS], diagonal[:, 0:STEPS, :], AX.X, ALU.add))
            v.tensor_copy(k_int[:, 0:STEPS], k_of_step[:, 0:STEPS]).then_inc(kint_ready, 1)

            dve.wait_ge(thr_turned, 1)
            link(v.tensor_copy(thr_i.rearrange("p (t c) -> p c t", t=T),
                               bank(0)[:, 0:TN].rearrange("p (c t) -> p c t", t=T)))
            link(v.tensor_scalar(lo_i, thr_i, P - 1, None, ALU.bitwise_and))
            link(v.tensor_scalar(hi_i, thr_i, 7, None, ALU.arith_shift_right))
            link(v.tensor_copy(lo_all[:, 0:TN], lo_i))
            link(v.tensor_copy(hi_all[:, 0:TN], hi_i))

            def digits(t):
                hi = hi_all[:, bass.ds(t * NB, NB)].rearrange("p (c h) -> p c h", h=1).broadcast_to([P, NB, NB])
                io = iota_h[:, :].rearrange("p (c h) -> p c h", c=1).broadcast_to([P, NB, NB])
                v.tensor_tensor(eq_hi[:, :, :], hi, io, ALU.is_equal)
                v.tensor_tensor(lt_hi[:, :, :], hi, io, ALU.is_lt)
                v.tensor_copy(lo_slot[:, :], lo_all[:, bass.ds(t * NB, NB)]).then_inc(digit_ready, 1)
                dve.wait_ge(digit_ready, t + 1)
                dve.sem_inc(dve_held, 1)

            def low_digit(c):
                return v.tensor_scalar(ge_lo[:, c, :], iota_l[:, :], lo_slot[:, c:c + 1], None, ALU.is_ge)

            def find_seg(par, t):
                dve.wait_ge(counts_ready, t + 1)
                v.tensor_scalar(seg[:, par, :], COUNTS, -1.0, None, ALU.add).then_inc(seg_ready, 1)

            digits(0)
            for c in range(NB):
                last = low_digit(c)
            last.then_inc(hot_ready, 1)
            find_seg(0, 0)

            def table_sums(par, t):
                ks = stair_registers(mybir.EngineType.DVE, t)
                dve.wait_ge(seg_ready, t + 1)
                dve.sem_inc(dve_held, 1)
                for u in range(BEATS):
                    s1 = beat_steps(u)[-1]
                    seen = STEPS * t + STEPS + (s1 - 16) + 1 if s1 >= 16 else STEPS * t + min(s1 + 16, STEPS - 1) + 1
                    dve.wait_ge(member_used, seen)
                    dve.sem_inc(dve_held, 1)
                    for s in beat_steps(u):
                        last = v.tensor_scalar(member[:, s % 16, :], iota_l[:, :], bag_base[:, bass.ds(ks[s] * -1 + s, 1)],
                                               seg[:, par, bass.ds(ks[s], 1)], ALU.add, ALU.is_equal)
                    last.then_inc(member_ready, 1)
                    if u == 0:
                        digits(t + 1)
                    for c in range(4 * u, min(4 * u + 4, NB)):
                        last = low_digit(c)
                    if u == 3:
                        last.then_inc(hot_ready, 1)
                find_seg(1 - par, t + 1)

            dve.wait_ge(krow_in, 16)
            with dve.Fori(0, T // 2) as it:
                for par in range(2):
                    table_sums(par, 2 * it + par)

            def stage(at, slot, first=0, end=FEA):
                stage_still(v.tensor_copy, at, slot, first, end)
                for half in range(2):
                    last = stage_moving(v.tensor_copy, at, slot, half, first, end)
                if end == FEA:
                    last.then_inc(staged, 1)

            dve.wait_ge(turned_read, T + 1)
            for batch in range(2):
                stage(GB * batch, batch, 0, T)
            dve.wait_ge(turned_read, T + 2)
            for batch in range(2):
                stage(GB * batch, batch, T)

            def chunk(c, slot, first, last):
                if not first:
                    dve.wait_ge(top_made, 7 * c - 3)
                for u in range(UNITS):
                    if u % 2 == 0 and not (first and u == 0) and not (last and u == UNITS - 2):
                        dve.wait_ge(gram_made, UNITS * c + u + 4)
                        stage(HCH * c + GB * (u // 2 + 1), (u // 2 + 1) % 2)
                    copy_unit(dve, v.tensor_copy, (3,), spare_dve, gram_dve, c, slot, u)

            each_chunk(dve, chunk)

        @block.scalar
        def _(act):
            a = nc.scalar

            def hand_indices(par, t, h):
                w = NB // 2
                a.copy(idx_slot[:, par, h * w:(h + 1) * w],
                       idx_all[:, bass.ds(t * NB + h * w, w)]).then_inc(slot_ready, 1)

            def mlp_tile(c, half, i):
                act.wait_ge(mlp_made, 7 * c + 7 * NCH // 2 * half + i + 1)
                src = bank(6 + i % 2)[:, 0:CH]
                if i < 4:
                    a.activation(hid0[:, i, :], src, ACT.Relu, bias=bias[:, cb0 + i:cb0 + i + 1]).then_inc(mlp_read, 1)
                elif i < 6:
                    a.activation(hid1[:, i - 4, :], src, ACT.Relu,
                                 bias=bias[:, cb1 + i - 4:cb1 + i - 3]).then_inc(mlp_read, 1)
                else:
                    a.activation(featT[D * half:D * half + D, bass.ds(c * CH, CH)], src[0:D, :],
                                 ACT.Relu, bias=bias[0:D, cb2:cb2 + 1]).then_inc(mlp_read, 1)

            def copy_turned(par, t):
                act.wait_ge(turned, t + 1)
                a.copy(featT[:, bass.ds(t * HALF, HALF)], bank(ACC[par], 2)).then_inc(turned_read, 1)

            def table(par, t, tiles={}, tile=None):
                def tiles_of(*beats):
                    for u in beats:
                        for i in tiles.get(u, []):
                            tile(i)

                tiles_of(0, 1)
                copy_turned(1 - par, t)
                tiles_of(2, 3, 4, 5)
                act.wait_ge(member_used, t * STEPS + STEPS + ROWS_LEFT)
                hand_indices(par, t + 2, 0)
                tiles_of(6, 7)
                act.wait_ge(member_used, t * STEPS + 2 * STEPS)
                hand_indices(par, t + 2, 1)
                a.copy(pooled.rearrange("p (j h d) -> p h j d", h=2, d=D),
                       bank(ACC[par], 2).rearrange("p (h j d) -> p h j d", h=2, d=D)).then_inc(acc_read, 1)

            act.wait_ge(idx_ready, 1)
            for par in range(2):
                for h in range(2):
                    hand_indices(par, par, h)
            act.wait_ge(w_in, W_IN)
            act.wait_ge(thr_turned, 1)
            with act.Fori(0, MLP_FROM) as it:
                for par in range(2):
                    table(par, 2 * it + par)
            for half in range(2):
                with act.Fori(0, NCH // 2 - half) as c:
                    for par in range(2):
                        table(par, 2 * c + (2 * MLP_FROM + NCH * half + par), MLP_TILES[par],
                              lambda i: mlp_tile(c, half, i))
            for par in range(2):
                table(par, T - 2 + par, LAST_TILES[par], lambda i: mlp_tile(NCH // 2 - 1, 1, i))
            mlp_tile(NCH // 2 - 1, 1, 5)
            copy_turned(1, T)
            mlp_tile(NCH // 2 - 1, 1, 6)

            def top_tile(c, slot, i):
                act.wait_ge(top_made, 7 * c + i + 8)
                if i < 4:
                    a.activation(top0[:, i, :], bank(i)[:, 0:CH], ACT.Relu,
                                 bias=bias[:, ct0 + i:ct0 + i + 1]).then_inc(top_read, 1)
                elif i < 6:
                    a.activation(top1[:, i - 4, :], bank(i - 4)[:, 0:CH], ACT.Relu,
                                 bias=bias[:, ct1 + i - 4:ct1 + i - 3]).then_inc(top_read, 1)
                else:
                    act.wait_ge(out_done[slot], 8 * c + (16 - 8 * slot))
                    a.activation(y_out[0:1, slot * CH:(slot + 1) * CH], bank(2)[0:1, 0:CH], ACT.Sigmoid,
                                 bias=bias[0:1, ct2:ct2 + 1]).then_inc(top_read, 1)

            def chunk(c, slot, first, last):
                if not first:
                    act.wait_ge(top_made, 7 * c - 3)
                for u in range(UNITS):
                    copy_unit(act, a.copy, (0, 1, 2), spare_act, gram_act, c, slot, u)
                    if u == UNITS - 2:
                        for half in range(2):
                            x = a.copy(z[D:P, slot, NJ - 1, half, :],
                                       featT[D * half:D * half + D, bass.ds(c * HCH, HCH)])
                        x.then_inc(x_placed, 1)
                    if u and not first:
                        top_tile(c - 1, 1 - slot, u - 1)

            each_chunk(act, chunk)
            for i in range(7):
                top_tile(NCH - 1, 1, i)

        @block.tensor
        def _(pe):
            mm = nc.tensor.matmul
            pe.sem_inc(member_used, STEPS)
            pe.sem_inc(turned_read, 1)
            pe.sem_inc(mlp_read, 1)
            pe.sem_inc(gram_made, 4)
            pe.sem_inc(gram_act, 2)
            pe.sem_inc(gram_dve, 2)
            pe.sem_inc(top_made, 7)
            pe.sem_inc(top_read, 7)
            pe.sem_inc(out_done[0], 16)
            pe.sem_inc(out_done[1], 16)

            pe.wait_ge(consts_ready, CONSTS)
            pe.wait_ge(thr_ready, 1)
            for c in range(NB):
                last = nc.tensor.transpose(bank(0)[:, c * T:(c + 1) * T], thr[:, c * P:(c + 1) * P], ident[0:T, 0:T])
            last.then_inc(thr_turned, 1)

            def count(t):
                pe.wait_ge(hot_ready, t + 1)
                for c in range(NB):
                    mm(COUNTS, ones[:, :], lt_hi[:, c, :], start=(c == 0), stop=False)
                for c in range(NB):
                    last = mm(COUNTS, ge_lo[:, c, :], eq_hi[:, c, :], start=False, stop=(c == NB - 1))
                last.then_inc(counts_ready, 1)

            count(0)

            def top_tile(c, slot, i):
                zc = z[:, slot].rearrange("p n h b -> p n (h b)")
                if i == 0:
                    pe.wait_ge(x_placed, c + 1)
                    pe.wait_ge(gram_act, UNITS * c + (UNITS + 2))
                    pe.wait_ge(gram_dve, UNITS * c + (UNITS + 2))
                if i < 4:
                    pe.wait_ge(top_read, 7 * c + (5, 6, 7, 4)[i])
                    dst = bank(i)[:, 0:CH]
                    pairs = [(wt0[:, n, i * P:(i + 1) * P], zc[:, n]) for n in range(NJ)]
                else:
                    pe.wait_ge(top_read, 7 * c + (11, 11, 13)[i - 4])
                    if i < 6:
                        dst = bank(i - 4)[:, 0:CH]
                        pairs = [(wt1[:, k, (i - 4) * P:(i - 3) * P], top0[:, k, :]) for k in range(Y0 // P)]
                    else:
                        dst = bank(2)[0:1, 0:CH]
                        pairs = [(wt2[:, k:k + 1], top1[:, k, :]) for k in range(Y1 // P)]
                for k, (weights, columns) in enumerate(pairs):
                    last = mm(dst, weights, columns, start=(k == 0), stop=(k == len(pairs) - 1))
                last.then_inc(top_made, 1)

            def mlp_tile(c, half, i):
                n7 = 7 * c + 7 * NCH // 2 * half
                pe.wait_ge(mlp_read, n7 + (1, 1, 2, 3, 5, 5, 7)[i])
                if i < 4:
                    pe.sem_inc(pe_held, 1)
                dst = bank(6 + i % 2)[:, 0:CH]
                if i < 4:
                    mm(dst, wb0[:, i * P:(i + 1) * P], x_sb[:, bass.ds(half * HALF + c * CH, CH)],
                       start=True, stop=True).then_inc(mlp_made, 1)
                elif i < 6:
                    for k in range(H0 // P):
                        last = mm(dst, wb1[:, k, (i - 4) * P:(i - 3) * P], hid0[:, k, :],
                                  start=(k == 0), stop=(k == H0 // P - 1))
                    last.then_inc(mlp_made, 1)
                else:
                    for k in range(H1 // P):
                        last = mm(dst[0:D, :], wb2[:, k, :], hid1[:, k, :], start=(k == 0), stop=(k == H1 // P - 1))
                    last.then_inc(mlp_made, 1)

            def turn(par, t):
                pe.wait_ge(acc_read, t + 1)
                for j in range(NB // 2):
                    last = nc.tensor.transpose(bank(ACC[par], 2)[:, j * P:(j + 1) * P],
                                               pooled[:, j * P:(j + 1) * P], ident[:, :])
                last.then_inc(turned, 1)

            def table(par, it, t, tiles={}, tile=None):
                ks = stair_registers(mybir.EngineType.PE, t)
                acc = ACC[par]
                pe.wait_ge(turned_read, t + 1)
                for h in range(2):
                    mm(bank(acc + h)[:, 0:D], zeros[:, :], zeros[:, 0:D], start=True, stop=False, skip_group_check=True)
                pe.wait_ge(rows_in[par][0], 128 * it + 128)
                for u in range(BEATS):
                    if u == 2:
                        turn(1 - par, t)
                        pe.wait_ge(rows_in[par][1], 128 * it + 128)
                    pe.wait_ge(member_ready, t * BEATS + u + 1)
                    for s in beat_steps(u):
                        mm(ps[:, bass.ds(ks[s] * -D + (s * D + acc * BANK), D)], member[:, s % 16, :],
                           rows[:, par, bass.ds(ks[s] * D, D)], start=False, stop=(s == STEPS - 1),
                           skip_group_check=True).then_inc(member_used, 1)
                    if u == 5:
                        count(t + 1)
                    for i in tiles.get(u, []):
                        tile(i)

            pe.wait_ge(krow_in, 16)
            pe.wait_ge(x_in, 64)
            pe.wait_ge(w_in, W_IN)
            with pe.Fori(0, MLP_FROM) as it:
                for par in range(2):
                    table(par, it, 2 * it + par)
            for half in range(2):
                it0 = MLP_FROM + NCH // 2 * half
                with pe.Fori(0, NCH // 2 - half) as c:
                    for par in range(2):
                        table(par, c + it0, 2 * c + (2 * it0 + par), MLP_TILES[par], lambda i: mlp_tile(c, half, i))
            for par in range(2):
                table(par, T // 2 - 1, T - 2 + par, LAST_TILES[par], lambda i: mlp_tile(NCH // 2 - 1, 1, i))
            mlp_tile(NCH // 2 - 1, 1, 5)
            turn(1, T)
            mlp_tile(NCH // 2 - 1, 1, 6)
            pe.wait_ge(zeros_ready, 1)
            pe.wait_ge(mlp_read, 7 * NCH + 1)

            def chunk(c, slot, first, last):
                for u in range(UNITS):
                    gram_unit(c, u)
                    if u and not first:
                        top_tile(c - 1, 1 - slot, u - 1)
                if first:
                    pe.wait_ge(top_in, 16)
                    pe.wait_ge(zeros_ready, 2)

            each_chunk(pe, chunk)
            for i in range(7):
                top_tile(NCH - 1, 1, i)


_INS = ["off", "idx", "tables", "xT", "Wb0", "bb0", "Wb1", "bb1", "Wb2", "bb2", "Wt0", "bt0", "Wt1", "bt1", "Wt2", "bt2"]


def kernel(r_dense_x, r_sparse_off, L0_rec_sparse_idx, L0_rec_emb_tables, L0_rec_W_bot0, L0_rec_b_bot0,
           L0_rec_W_bot1, L0_rec_b_bot1, L0_rec_W_bot2, L0_rec_b_bot2, L0_rec_W_top0, L0_rec_b_top0,
           L0_rec_W_top1, L0_rec_b_top1, L0_rec_W_top2, L0_rec_b_top2):
    import numpy as np
    import concourse.bacc as bacc
    from concourse.bass_utils import run_bass_kernel_spmd as run

    def column(vec, w):
        return np.ascontiguousarray(np.asarray(vec).reshape(-1, w).T)

    w0 = np.asarray(L0_rec_W_top0)
    wt0 = np.zeros((P, NJ, Y0), w0.dtype)
    row = D
    for i in range(FEA):
        for j in range(i + 1, FEA):
            n, m = divmod(j - 1 - PAD, QUAD)
            at = (32 * m + i, n) if j > PAD else (FEA + i, j - 1)
            wt0[at] = w0[row]
            row += 1
    wt0[D:P, NJ - 1] = w0[0:D]
    data = {
        "off": np.asarray(r_sparse_off),
        "idx": np.ascontiguousarray(np.asarray(L0_rec_sparse_idx).reshape(T, NB, P).transpose(2, 0, 1).reshape(P, T * NB)),
        "tables": np.asarray(L0_rec_emb_tables),
        "xT": np.ascontiguousarray(np.asarray(r_dense_x).T),
        "Wb0": np.asarray(L0_rec_W_bot0), "bb0": column(L0_rec_b_bot0, P),
        "Wb1": np.asarray(L0_rec_W_bot1), "bb1": column(L0_rec_b_bot1, P),
        "Wb2": np.asarray(L0_rec_W_bot2), "bb2": column(L0_rec_b_bot2, D),
        "Wt0": wt0, "bt0": column(L0_rec_b_top0, P),
        "Wt1": np.asarray(L0_rec_W_top1), "bt1": column(L0_rec_b_top1, P),
        "Wt2": column(L0_rec_W_top2, P), "bt2": column(L0_rec_b_top2, 1),
    }
    nc = bacc.Bacc("TRN2", target_bir_lowering=False, num_devices=1)
    args = [nc.dram_tensor(n, data[n].shape, mybir.dt.from_np(data[n].dtype), kind="ExternalInput").ap() for n in _INS]
    out = nc.dram_tensor("out", (1, B), F32, kind="ExternalOutput").ap()
    build(nc, *args, out)
    result = run(nc, [data], core_ids=[0])
    return result.results[0]["out"].reshape(B)
```
